# Optimizing a Trainium2 kernel written in Bass

```python
import numpy as np
import jax
import jax.numpy as jnp

def _softmax(x, axis=-1):
    return jax.nn.softmax(x, axis=axis)

def _gelu(x):
    return jax.nn.gelu(x, approximate=True)

def _silu(x):
    return jax.nn.silu(x)

def _sigmoid(x):
    return jax.nn.sigmoid(x)

def _layernorm(x, axis=-1, eps=1e-05):
    m = jnp.mean(x, axis=axis, keepdims=True)
    v = jnp.var(x, axis=axis, keepdims=True)
    return (x - m) / jnp.sqrt(v + eps)

def _scatter_add(tgt, idx, src, axis=0):
    return tgt.at[idx].add(src)

def _segment_sum(src, seg, n):
    return jax.ops.segment_sum(src, seg, n)
kernel_name = 'mk_xattn_ffn_d1_seqx_r2_a4c3f5'

def setup_inputs(seed: int=0):
    np.random.seed(seed)
    _w = jnp.asarray

    def _rec_inputs():
        import jax
        import jax.numpy as jnp
        _rk = jax.random.key(seed)
        x = -0.0003929 + 0.9999 * jax.random.normal(jax.random.fold_in(_rk, 1), (16, 256, 512), jnp.float32)
        _lenS = 256 - jax.random.randint(jax.random.fold_in(_rk, 7), (16,), 0, max(1, 256 // 4) + 1, jnp.int32)
        _lenS2 = 256 - jax.random.randint(jax.random.fold_in(_rk, 8), (16,), 0, max(1, 256 // 4) + 1, jnp.int32)
        _ctx_768P = jax.random.normal(jax.random.fold_in(_rk, 11), (16, 16, 384), jnp.float32)
        _ctx_768c = jax.random.dirichlet(jax.random.fold_in(_rk, 511), 0.3 * jnp.ones((16,), jnp.float32), (16, 256))
        _ctx_768t = jnp.einsum('bsk,bkd->bsd', _ctx_768c, _ctx_768P)
        _ctx_768t = _ctx_768t * jax.lax.rsqrt(jnp.mean(jnp.square(_ctx_768t)) + 1e-12) * 0.953939
        ctx_768 = -7.36909e-05 + 0.999899 * (_ctx_768t + 0.3 * jax.random.normal(jax.random.fold_in(_rk, 611), (16, 256, 384), jnp.float32))
        return (x, ctx_768)
    x, ctx_768 = _rec_inputs()

    def _L0_xattn_setup():
        import jax, jax.numpy as jnp
        import numpy as np
        EPS = 1e-05

        def layernorm(x, g, b):
            mu = jnp.mean(x, axis=-1, keepdims=True)
            var = jnp.mean(jnp.square(x - mu), axis=-1, keepdims=True)
            return (x - mu) * jax.lax.rsqrt(var + EPS) * g + b
        key = jax.random.key(seed)
        ks = jax.random.split(key, 12)
        B, L1, L2 = (8, 1024, 1024)
        D1, D2, E = (512, 384, 512)
        s1, s2, se = (D1 ** (-0.5), D2 ** (-0.5), E ** (-0.5))
        return {'modality1': jax.random.normal(ks[0], (B, L1, D1), jnp.float32), 'modality2': jax.random.normal(ks[1], (B, L2, D2), jnp.float32), 'ln1_g': jnp.ones((D1,), jnp.float32), 'ln1_b': jnp.zeros((D1,), jnp.float32), 'ln2_g': jnp.ones((D2,), jnp.float32), 'ln2_b': jnp.zeros((D2,), jnp.float32), 'Wq': jax.random.normal(ks[2], (D1, E), jnp.float32) * s1, 'bq': jax.random.normal(ks[3], (E,), jnp.float32) * 0.01, 'Wk': jax.random.normal(ks[4], (D2, E), jnp.float32) * s2, 'bk': jax.random.normal(ks[5], (E,), jnp.float32) * 0.01, 'Wv': jax.random.normal(ks[6], (D2, E), jnp.float32) * s2, 'bv': jax.random.normal(ks[7], (E,), jnp.float32) * 0.01, 'Wo': jax.random.normal(ks[8], (E, D1), jnp.float32) * se, 'bo': jax.random.normal(ks[9], (D1,), jnp.float32) * 0.01}
    _L0_xattn_all = _L0_xattn_setup()
    _L0_xattn_in = {k: v for k, v in _L0_xattn_all.items() if k in ('ln1_g', 'ln1_b', 'ln2_g', 'ln2_b', 'Wq', 'bq', 'Wk', 'bk', 'Wv', 'bv', 'Wo', 'bo')}
    del _L0_xattn_all

    def _L0_ffn_setup():
        import jax, jax.numpy as jnp
        import numpy as np

        def _bitlinear(x, w_latent):
            scale = jax.lax.stop_gradient(jnp.clip(jnp.mean(jnp.abs(w_latent), axis=1, keepdims=True), 1e-05, None))
            tern = jnp.clip(jnp.round(w_latent / scale), -1.0, 1.0)
            w = w_latent + jax.lax.stop_gradient(tern - w_latent)
            return x @ (w * scale).T
        key = jax.random.key(seed)
        ks = jax.random.split(key, 6)
        dim, hidden, rank = (512, 2048, 16)
        B, S = (4, 2048)
        x = jax.random.normal(ks[0], (B, S, dim), dtype=jnp.float32)
        w_fc = 0.02 * jax.random.normal(ks[1], (hidden, dim), dtype=jnp.float32)
        w_proj = 0.02 * jax.random.normal(ks[2], (dim, hidden), dtype=jnp.float32)
        u = 0.02 * jax.random.normal(ks[3], (hidden, rank), dtype=jnp.float32)
        v = 0.02 * jax.random.normal(ks[4], (rank, dim), dtype=jnp.float32)
        fast_b = jax.random.normal(ks[5], (rank, rank), dtype=jnp.float32)
        gate = jnp.float32(0.05)
        return {'x': x, 'fast_b': fast_b, 'w_fc': w_fc, 'w_proj': w_proj, 'u': u, 'v': v, 'gate': gate}
    _L0_ffn_all = _L0_ffn_setup()
    _L0_ffn_in = {k: v for k, v in _L0_ffn_all.items() if k in ('fast_b', 'w_fc', 'w_proj', 'u', 'v', 'gate')}
    del _L0_ffn_all
    return {'x': x, 'ctx_768': ctx_768, 'L0_xattn_ln1_g': _L0_xattn_in['ln1_g'], 'L0_xattn_ln1_b': _L0_xattn_in['ln1_b'], 'L0_xattn_ln2_g': _L0_xattn_in['ln2_g'], 'L0_xattn_ln2_b': _L0_xattn_in['ln2_b'], 'L0_xattn_Wq': _L0_xattn_in['Wq'], 'L0_xattn_bq': _L0_xattn_in['bq'], 'L0_xattn_Wk': _L0_xattn_in['Wk'], 'L0_xattn_bk': _L0_xattn_in['bk'], 'L0_xattn_Wv': _L0_xattn_in['Wv'], 'L0_xattn_bv': _L0_xattn_in['bv'], 'L0_xattn_Wo': _L0_xattn_in['Wo'], 'L0_xattn_bo': _L0_xattn_in['bo'], 'L0_ffn_fast_b': _L0_ffn_in['fast_b'], 'L0_ffn_w_fc': _L0_ffn_in['w_fc'], 'L0_ffn_w_proj': _L0_ffn_in['w_proj'], 'L0_ffn_u': _L0_ffn_in['u'], 'L0_ffn_v': _L0_ffn_in['v'], 'L0_ffn_gate': _L0_ffn_in['gate']}

def reference(x, ctx_768, L0_xattn_ln1_g, L0_xattn_ln1_b, L0_xattn_ln2_g, L0_xattn_ln2_b, L0_xattn_Wq, L0_xattn_bq, L0_xattn_Wk, L0_xattn_bk, L0_xattn_Wv, L0_xattn_bv, L0_xattn_Wo, L0_xattn_bo, L0_ffn_fast_b, L0_ffn_w_fc, L0_ffn_w_proj, L0_ffn_u, L0_ffn_v, L0_ffn_gate):
    import jax
    import jax.numpy as jnp

    def _L0_xattn_ref(modality1, modality2, ln1_g, ln1_b, ln2_g, ln2_b, Wq, bq, Wk, bk, Wv, bv, Wo, bo):
        import jax, jax.numpy as jnp
        import numpy as np
        EPS = 1e-05

        def layernorm(x, g, b):
            mu = jnp.mean(x, axis=-1, keepdims=True)
            var = jnp.mean(jnp.square(x - mu), axis=-1, keepdims=True)
            return (x - mu) * jax.lax.rsqrt(var + EPS) * g + b
        E = Wq.shape[1]
        scaling = E ** (-0.5)
        x1 = layernorm(modality1, ln1_g, ln1_b)
        x2 = layernorm(modality2, ln2_g, ln2_b)
        q = x1 @ Wq + bq
        k = x2 @ Wk + bk
        v = x2 @ Wv + bv
        scores = jnp.einsum('bqe,bke->bqk', q, k) * scaling
        attn = jax.nn.softmax(scores, axis=-1)
        ctx = jnp.einsum('bqk,bke->bqe', attn, v)
        return ctx @ Wo + bo

    def _L0_ffn_ref(x, fast_b, w_fc, w_proj, u, v, gate):
        import jax, jax.numpy as jnp
        import numpy as np

        def _bitlinear(x, w_latent):
            scale = jax.lax.stop_gradient(jnp.clip(jnp.mean(jnp.abs(w_latent), axis=1, keepdims=True), 1e-05, None))
            tern = jnp.clip(jnp.round(w_latent / scale), -1.0, 1.0)
            w = w_latent + jax.lax.stop_gradient(tern - w_latent)
            return x @ (w * scale).T
        h = _bitlinear(x, w_fc) + gate * (x @ v.T @ fast_b.T @ u.T)
        r = jnp.maximum(h, 0.0)
        return _bitlinear(r * r, w_proj)
    x = x + _L0_xattn_ref(_layernorm(x, axis=-1), ctx_768, L0_xattn_ln1_g, L0_xattn_ln1_b, L0_xattn_ln2_g, L0_xattn_ln2_b, L0_xattn_Wq, L0_xattn_bq, L0_xattn_Wk, L0_xattn_bk, L0_xattn_Wv, L0_xattn_bv, L0_xattn_Wo, L0_xattn_bo)
    x = x + _L0_ffn_ref(_layernorm(x, axis=-1), L0_ffn_fast_b, L0_ffn_w_fc, L0_ffn_w_proj, L0_ffn_u, L0_ffn_v, L0_ffn_gate)
    return x

_drawn_inputs = setup_inputs


def setup_inputs(seed=0):
    import zlib

    import numpy as np

    out = dict(_drawn_inputs(seed))
    spreads = {'L0_xattn_ln1_g': (1.0, 0.2),
     'L0_xattn_ln1_b': (0.0, 0.524),
     'L0_xattn_ln2_g': (1.0, 0.2),
     'L0_xattn_ln2_b': (0.0, 0.1)}
    factors = {'L0_xattn_bq': 29.161,
     'L0_xattn_bk': 64.0,
     'L0_xattn_bv': 7.08,
     'L0_xattn_bo': 6.797,
     'L0_ffn_fast_b': 8.0,
     'L0_ffn_u': 8.0,
     'L0_ffn_v': 8.0}
    for name, (base, spread) in spreads.items():
        noise = np.random.default_rng([zlib.crc32(name.encode()), seed]).standard_normal(out[name].shape)
        drawn = base * np.exp(spread * noise) if base else spread * noise
        out[name] = jnp.asarray(drawn.astype(out[name].dtype))
    for name, factor in factors.items():
        out[name] = (out[name] * factor).astype(out[name].dtype)
    return out
```

```python
from contextlib import ExitStack

import concourse.bass as bass
from concourse import mybir

P = 128
ALU = mybir.AluOpType
ACT = mybir.ActivationFunctionType
F32 = mybir.dt.float32
F32R = mybir.dt.float32r
BF16 = mybir.dt.bfloat16
AX_X = mybir.AxisListType.X
HI, LO = 0, 1
EPS = 1e-5

TILES = 4
TOK = TILES * P
NPRE = 25
NBODY = 30
NROOT = 6
NFF = 16

ATTENTION = ([("n1T", t) for t in range(4)] + [("n2T", t) for t in range(4)]
             + [("t", 0), ("t", 1), ("t", 2), ("s", 0), ("s", 1), ("v", 0), ("v", 1), ("pT", 0),
                ("s", 2), ("s", 3), ("v", 2), ("v", 3), ("a", 0), ("a", 1), ("pT", 1), ("a", 2), ("a", 3)])
BODY = [("x", 0), ("x", 1), ("x", 2), ("x", 3), ("L", 0)] + ATTENTION
assert len(ATTENTION) == NPRE and len(BODY) == NBODY


def unit_list(b):
    return ATTENTION if isinstance(b, int) and b < 0 else BODY


def units_before(b, kept):
    if isinstance(b, int) and b < 0:
        return 0
    return b * sum(map(kept, BODY)) + sum(map(kept, ATTENTION))


def count(b, unit, kept=lambda u: True):
    seq = unit_list(b)
    return units_before(b, kept) + sum(map(kept, seq[:seq.index(unit) + 1]))


def on_act(unit):
    return unit[0] != "a"


def n_full(b, unit):
    return count(b, unit)


def n_act(b, unit):
    return count(b, unit, on_act)


def n_dve(b, unit):
    return count(b, unit)


def bank_of(b, unit):
    if unit == ("x", 2):
        return "H0"
    if unit == ("x", 3):
        return "H1"
    return f"G{unit_list(b).index(unit) % 2}"


def bank_before(b, unit):
    seq, bank = unit_list(b), bank_of(b, unit)
    for u in reversed(seq[:seq.index(unit)]):
        if bank_of(b, u) == bank:
            return b, u
    if isinstance(b, int) and b < 0:
        return None
    for u in reversed(unit_list(b - 1)):
        if bank_of(b - 1, u) == bank:
            return b - 1, u


PLACED = {
    0: ["xstats", "nx0"], 1: ["nx1", ("n1T", 0)], 2: [("n1T", 1), "nx2", "cstats"], 3: [("n1T", 2), "nx3", "nc0"],
    4: [("n1T", 3), "nc1", "nc2"], 5: [("n2T", 0), "nc3"], 6: [("n2T", 1)], 7: [("n2T", 2)], 8: [("n2T", 3)],
    10: [("t", 0)], 11: [("t", 1)], 12: [("t", 2)], 14: [("s", 0)], 15: [("s", 1)], 16: [("v", 0)],
    17: [("v", 1)], 18: [("pT", 0)], 19: [("s", 2)], 20: [("s", 3)], 21: [("v", 2)], 22: [("v", 3)],
    23: [("a", 0), "nX0"], 24: [("a", 1), "nX1"], 25: [("pT", 1)], 27: [("a", 2)], 28: [("a", 3)],
}
assert [s for h in sorted(PLACED) for s in PLACED[h] if isinstance(s, tuple)] == ATTENTION


def body_steps(attention, leftover):
    out = [("x", 0), "nX2", ("x", 1), "nX3"]
    if leftover:
        out += [("down-", NFF - 2)]
    out += [("x", 2), ("x", 3)]
    if leftover:
        out += [("down-", NFF - 1)]
    out += [("L", 0)]
    for j in range(NFF):
        out += [("up", j)]
        if j == 0 and leftover:
            out += ["out"]
        if j == 0 and attention:
            out += ["residual", "load"]
        out += PLACED.get(2 * j, []) if attention else []
        out += [("sq", j), ("hi", j)]
        if j >= 2:
            out += [("down", j - 2)]
        out += PLACED.get(2 * j + 1, []) if attention else []
        out += [("lo", j)]
    return out


def prologue_steps():
    out = ["xstats", "cstats", "nx0", "nx1", "nc0", "nc1", "nc2", "nc3"]
    slots = [[u] for u in ATTENTION]
    for s in slots:
        if s[0] in (("n1T", 0), ("n1T", 1)):
            s.append(f"nx{s[0][1] + 2}")
        if s[0] in (("a", 0), ("a", 1)):
            s.append(f"nX{s[0][1]}")
    slots[0].append("residual")
    slots[8].append("load")
    pieces = []
    for g in range(8):
        pieces += [("abs", g), ("scale", g)] + [("piece", 4 * g + i) for i in range(4)]
        if g == 4:
            pieces += ["uprep"] + [("ut", i) for i in range(4)]
    done = 0
    for n, s in enumerate(slots):
        want = len(pieces) * (n + 1) // len(slots)
        out += s + pieces[done:want]
        done = want
    return out + ["sprow"]


def mk_xattn_ffn(nc, x, ctx_768, ln1_g, ln1_b, ln2_g, ln2_b, Wq, bq, Wk, bk, Wv, bv, Wo, bo,
                 fast_b, w_fc, w_proj, u, v, gate, out):
    NB, S, D = x.shape
    DC = ctx_768.shape[2]
    E = Wq.shape[1]
    HID = w_fc.shape[0]
    RK = fast_b.shape[0]
    KD, KC, KE = D // P, DC // P, E // P
    NG = NB * S // TOK
    assert S == 256 and D == 512 and E == 512 and HID == NFF * P and RK == 16 and NG == 8
    SM = float(E) ** -0.5

    x_in = x.rearrange("(g c) (p t) d -> g p c (t d)", c=2, t=2)
    ctx_in = ctx_768.rearrange("(g c) (p t) d -> g p c (t d)", c=2, t=2)
    out_v = out.rearrange("(g c) (p t) d -> g c p (t d)", c=2, t=2)

    with ExitStack() as stack:
        def sb(name, shape, dt=F32, where=stack):
            return where.enter_context(nc.sbuf_tensor(name, shape, dt))

        def sem(name):
            return stack.enter_context(nc.semaphore(name))

        fcT = sb("fcT", [P, KD, HID], F32R)
        projT = sb("projT", [P, NFF, D], F32R)
        M = sb("M", [P, 2, KD, DC], F32R)
        Wvo = sb("Wvo", [P, 2, KC, D], F32R)
        uT = sb("uT", [P, HID], F32R)
        FB = sb("FB", [P, KD, P], F32R)
        ident = sb("ident", [P, P])
        identb = sb("identb", [P, P], BF16)
        sprow = sb("sprow", [P, D])
        crow = sb("crow", [P, D])
        tbias = sb("tbias", [P, KC])
        scf = sb("scf", [P, NFF])
        half = sb("half", [P, 2, 4])
        nhalf = sb("nhalf", [P, 2, 4])
        spc = sb("spc", [P, KD])
        asum = sb("asum", [P, 8, 4])
        psum4 = sb("psum4", [P, 4])
        urs = sb("urs", [P, NFF])
        g1c = sb("g1c", [P, KD])
        b1c = sb("b1c", [P, KD])
        g2c = sb("g2c", [P, KC])
        b2c = sb("b2c", [P, KC])
        bqc = sb("bqc", [P, KE])
        bvc = sb("bvc", [P, KE])
        bqp = sb("bqp", [P, KE])
        bvp = sb("bvp", [P, KE])
        gatec = sb("gatec", [P, 1])
        xst = sb("xst", [P, TILES, 6])
        xmv = sb("xmv", [P, TILES, 2])
        xrs = sb("xrs", [P, TILES])
        cst = sb("cst", [P, TILES, 6])
        cmv = sb("cmv", [P, TILES, 2])
        crs = sb("crs", [P, TILES])
        mhalf = sb("mhalf", [P, TILES])
        spare = sb("spare", [P, 1])
        nst = sb("nst", [P, TILES, 6])
        nmv = sb("nmv", [P, TILES, 2])
        nrs = sb("nrs", [P, TILES])
        rowmax = sb("rowmax", [P, TILES])
        nmax = sb("nmax", [P, TILES])
        rowsum = sb("rowsum", [P, TILES])
        rinv = sb("rinv", [P, TILES])
        ctxb = sb("ctxb", [P, TILES, DC])
        xb = sb("xb", [P, TILES, D])
        pbuf = sb("pbuf", [P, TILES, S])
        nrm = sb("nrm", [P, 2, D])
        tstack = sb("tstack", [P, TOK], F32R)
        x2a = sb("x2a", [P, TILES, D])
        yb = pbuf[:, :, :].rearrange("p (y h) s -> p y (h s)", y=2)

        setup = ExitStack()
        wring = sb("wring", [P, 2, 4, D], F32, setup)
        Wq_s = sb("Wq_s", [P, KD, E], F32, setup)
        Wk_s = sb("Wk_s", [P, KC, E], F32, setup)
        WqT = sb("WqT", [P, KE, D], F32, setup)
        Wv_s = sb("Wv_s", [P, KC, E], F32, setup)
        WkT = sb("WkT", [P, KE, DC], F32, setup)
        Wo_s = sb("Wo_s", [P, KE, D], F32, setup)
        WvT = sb("WvT", [P, KE, DC], F32, setup)
        tern = sb("tern", [P, 4, D], BF16, setup)
        unat = sb("unat", [P, NFF, 8, RK], F32, setup)
        ones = sb("ones", [P, P], F32, setup)
        bvrep = sb("bvrep", [P, KE, P], F32, setup)
        below = sb("below", [P, 2, D], BF16, setup)
        absj = sb("absj", [P, 2, D], BF16, setup)
        u_s = sb("u_s", [P, NFF, RK], F32, setup)
        fbT4 = sb("fbT4", [RK, 4, RK], F32, setup)
        uhi = sb("uhi", [P, NFF, RK], F32R, setup)
        setup.close()
        xnT = sb("xnT", [P, 2, KD, TOK], F32R)
        n1T = sb("n1T", [P, 2, KD, TOK], F32R)
        n2T = sb("n2T", [P, 2, KC, TOK], F32R)
        tT = sb("tT", [P, 2, KC, TOK], F32R)
        pT = sb("pT", [P, 2, 2, 2, S], F32R)
        rbuf = sb("rbuf", [P, 2, TOK])
        x2b = sb("x2b", [P, TILES, D])
        qbuf = sb("qbuf", [P, 2, 2, TOK], F32R)
        vo = n1T
        x2 = [x2a, x2b]
        v_s = nrm[0:RK, 0, :]
        borow = nrm[:, 1, :]

        banks = {n: stack.enter_context(nc.psum_tensor(n, [P, 512], F32))
                 for n in ("G0", "G1", "H0", "H1", "O0", "O1", "O2", "O3")}

        params_in = sem("params_in")
        wq_in, wk_in, wv_in, wo_in = sem("wq_in"), sem("wk_in"), sem("wv_in"), sem("wo_in")
        x_in_s, ctx_in_s = sem("x_loaded"), sem("ctx_loaded")
        ring_in = [sem("ring_in0"), sem("ring_in1")]
        stored = sem("stored")
        const_ready = sem("const_ready")
        job_full = sem("job_full")
        job_act = sem("job_act")
        job_dve = sem("job_dve")
        own = sem("dve_chain")
        pool_own = sem("pool_chain")
        abs_done = sem("abs_done")
        scales_made = sem("scales_made")
        tern_made = sem("tern_made")
        tern_turned = sem("tern_turned")
        tern_stored = sem("tern_stored")
        unat_made = sem("unat_made")
        ut_full = sem("ut_full")
        ut_stored = sem("ut_stored")
        diag_made = sem("diag_made")
        sprow_full = sem("sprow_full")
        unit_full = sem("unit_full")
        unit_act = sem("unit_act")
        unit_dve = sem("unit_dve")
        var_made = sem("var_made")
        rstd_made = sem("rstd_made")
        n1_made = sem("n1_made")
        n2_made = sem("n2_made")
        xn_made = sem("xn_made")
        res_made = sem("residual_made")
        up_full = sem("up_full")
        relu_made = sem("relu_made")
        square_made = sem("square_made")
        sqhi_made = sem("square_hi_made")
        sqlo_made = sem("square_lo_made")
        down_full = sem("down_full")
        y_made = sem("y_made")
        y_added = sem("y_added")

        JOBS = ([("wqT", c) for c in range(KD)] + [("wkT", c) for c in range(KC)]
                + [("wvT", c) for c in range(KC)] + [("bq", 0), ("bv", 0)]
                + [("M", c) for c in range(KD)] + [("tb", 0)] + [("wvo", c) for c in range(KC)]
                + [("co", 0), ("fb", 0)])
        JBANK = ["O0", "O1", "O2", "O3", "H0", "H1"]

        def job_engines(n):
            kind = JOBS[n][0]
            if kind in ("wqT", "wkT", "wvT"):
                return ("act",) if n % 2 == 0 else ("dve",)
            return ("act", "dve") if kind in ("M", "wvo", "fb") else ("dve",)

        def job_count(n, engine):
            return sum(engine in job_engines(i) for i in range(n + 1))

        def job_read(e, n):
            last = job_engines(n)[-1]
            e.wait_ge(job_act if last == "act" else job_dve, job_count(n, last))

        PIECES = 2 * NFF
        bodies = dict(attention=True, leftover=True)

        def run_bodies(e, steps):
            steps(-1, prologue_steps())
            steps(0, body_steps(True, False))
            with e.Fori(0, (NG - 2) // 2) as pair:
                for odd in (1, 0):
                    steps(2 * pair + 2 - odd, body_steps(True, True), (odd + 1) % 2 if False else odd)
            steps(NG - 1, body_steps(False, True))

        block = stack.enter_context(nc.Block())

        @block.sync
        def _(sp):
            sp.dma_start(Wq_s[:, :, :], Wq.rearrange("(c p) e -> p c e", p=P)).then_inc(wq_in, 16)
            sp.dma_start(Wk_s[:, :, :], Wk.rearrange("(c p) e -> p c e", p=P)).then_inc(wk_in, 16)
            sp.dma_start(xb[:, :, :].rearrange("p (c t) d -> p c (t d)", c=2), x_in[0]).then_inc(x_in_s, 16)
            sp.dma_start(ctxb[:, :, :].rearrange("p (c t) d -> p c (t d)", c=2), ctx_in[0]).then_inc(ctx_in_s, 16)
            sp.dma_start(Wv_s[:, :, :], Wv.rearrange("(c p) e -> p c e", p=P)).then_inc(wv_in, 16)
            sp.dma_start(Wo_s[:, :, :], Wo.rearrange("(c p) e -> p c e", p=P)).then_inc(wo_in, 16)

            def ring_load(g):
                src = (w_fc.rearrange("(g c p) d -> g p c d", c=4, p=P)[g] if g < 4
                       else w_proj.rearrange("(t p) (c d) -> t p c d", p=P, d=D)[g - 4])
                sp.dma_start(wring[:, g % 2, :, :], src).then_inc(ring_in[g % 2], 16)

            def load_next(b):
                sp.wait_ge(n1_made, 4 * (b + 2))
                sp.wait_ge(res_made, 4 * (b + 2))
                sp.dma_start(xb[:, :, :].rearrange("p (c t) d -> p c (t d)", c=2), x_in[b + 2]).then_inc(x_in_s, 16)
                sp.wait_ge(unit_full, n_full(b, ("n2T", 3)))
                sp.dma_start(ctxb[:, :, :].rearrange("p (c t) d -> p c (t d)", c=2), ctx_in[b + 2]).then_inc(ctx_in_s, 16)

            def store(g, tiles_of):
                for c in range(2):
                    sp.wait_ge(y_added, 4 * g + 2 * c + 2)
                    sp.dma_start(out_v[g, c], x2[tiles_of][:, 2 * c:2 * c + 2, :].rearrange("p t d -> p (t d)")
                                 ).then_inc(stored, 16)

            ring_load(0)
            ring_load(1)
            for g in range(2, 5):
                sp.wait_ge(tern_made, 4 * (g - 1))
                ring_load(g)
            load_next(-1)
            for g in range(5, 8):
                sp.wait_ge(tern_made, 4 * (g - 1))
                ring_load(g)
            load_next(0)
            with sp.Fori(0, 2) as pair:
                for odd in (1, 0):
                    store(2 * pair + 1 - odd, 1 - odd)
                    load_next(2 * pair + 2 - odd)
            store(4, 0)
            load_next(5)
            store(5, 1)
            store(6, 0)
            store(7, 1)
            sp.wait_ge(stored, 32 * NG)

        @block.gpsimd
        def _(pool):
            nc.gpsimd.memset(ident[:, :], 0.0).then_inc(pool_own, 1)
            pool.wait_ge(pool_own, 1)
            nc.gpsimd.affine_select(out=ident[:, :], in_=ident[:, :], compare_op=ALU.not_equal, fill=1.0, base=0,
                                    pattern=[[-1, P]], channel_multiplier=1).then_inc(pool_own, 1)
            nc.gpsimd.memset(ones[:, :], 1.0).then_inc(const_ready, 1)
            nc.gpsimd.memset(mhalf[:, :], -0.5).then_inc(pool_own, 1)
            pool.wait_ge(pool_own, 3)
            nc.gpsimd.tensor_copy(identb[:, :], ident[:, :]).then_inc(const_ready, 1)

            def steps(b, todo, odd=None):
                g = b + 1
                par = 0 if isinstance(b, int) and b < 0 else (odd + 1) % 2 if odd is not None else (b + 1) % 2
                for st in todo:
                    roots = {"xstats": (0, xrs[:, :]), "cstats": (1, crs[:, :])}
                    roots.update({("a", t): (2 + t, nrs[:, t:t + 1]) for t in range(TILES)})
                    if st in roots:
                        n, var = roots[st]
                        pool.wait_ge(var_made, NROOT * g + n + 1)
                        nc.gpsimd.tensor_tensor(var, var, mhalf[:, 0:var.shape[1]], ALU.pow).then_inc(rstd_made, 1)
                    elif st == "residual":
                        pool.wait_ge(x_in_s, 16 * (g + 1))
                        if isinstance(b, int) and b < 0:
                            pool.wait_ge(job_dve, job_count(len(JOBS) - 1, "dve"))
                        elif isinstance(b, int) and b == 0:
                            pool.wait_ge(ut_full, 4)
                        else:
                            pool.wait_ge(stored, 32 * b)
                        for t in range(TILES):
                            nc.gpsimd.tensor_tensor(x2[par][:, t, :], xb[:, t, :], crow[:, :],
                                                    ALU.add).then_inc(res_made, 1)
                    elif st == "out":
                        for t in range(TILES):
                            pool.wait_ge(y_made, 4 * (b - 1) + t + 1)
                            nc.gpsimd.tensor_tensor(x2[par][:, t, :], x2[par][:, t, :], yb[:, t % 2, :],
                                                    ALU.add).then_inc(y_added, 1)
            run_bodies(pool, steps)
            for t in range(TILES):
                pool.wait_ge(y_made, 4 * (NG - 1) + t + 1)
                nc.gpsimd.tensor_tensor(x2[1][:, t, :], x2[1][:, t, :], yb[:, t % 2, :], ALU.add).then_inc(y_added, 1)

        @block.scalar
        def _(act):
            small = [(g1c, ln1_g), (b1c, ln1_b), (g2c, ln2_g), (b2c, ln2_b), (bqc, bq), (bvc, bv)]
            for dst, src in small:
                act.dma_start(dst[:, :], src.rearrange("(c p) -> p c", p=P), allow_slow_non_contiguous=True).then_inc(params_in, 16)
            act.dma_start(gatec[:, :], gate.partition_broadcast(P)).then_inc(params_in, 16)
            act.dma_start(borow, bo.partition_broadcast(P)).then_inc(params_in, 16)
            act.dma_start(v_s, v).then_inc(params_in, 16)
            for i in range(4):
                act.dma_start(fbT4[:, i, :], fast_b.rearrange("r s -> s r"), allow_slow_non_contiguous=True).then_inc(params_in, 16)
            act.dma_start(u_s[:, :, :], u.rearrange("(c p) r -> p c r", p=P)).then_inc(params_in, 16)

            for n, (kind, c) in enumerate(JOBS):
                if "act" not in job_engines(n):
                    continue
                bank = banks[JBANK[n % 6]]
                act.wait_ge(job_full, n + 1)
                if kind == "wqT":
                    nc.scalar.activation(WqT[:, :, c * P:(c + 1) * P], bank[:, :].rearrange("p (k n) -> p k n", k=KE),
                                         ACT.Copy).then_inc(job_act, 1)
                elif kind == "wkT":
                    nc.scalar.activation(WkT[:, :, c * P:(c + 1) * P], bank[:, :].rearrange("p (k n) -> p k n", k=KE),
                                         ACT.Copy).then_inc(job_act, 1)
                elif kind == "wvT":
                    nc.scalar.activation(WvT[:, :, c * P:(c + 1) * P], bank[:, :].rearrange("p (k n) -> p k n", k=KE),
                                         ACT.Copy).then_inc(job_act, 1)
                elif kind == "M":
                    act.wait_ge(params_in, 16 * 14)
                    nc.scalar.activation(M[:, HI, c, :], bank[:, 0:DC], ACT.Copy, scale=g1c[:, c:c + 1]
                                         ).then_inc(job_act, 1)
                elif kind == "wvo":
                    nc.scalar.activation(Wvo[:, HI, c, :], bank[:, :], ACT.Copy, scale=g2c[:, c:c + 1]
                                         ).then_inc(job_act, 1)
                elif kind == "fb":
                    nc.scalar.activation(FB[:, :, 0:64], bank[:, 0:KD * 64].rearrange("p (k n) -> p k n", k=KD),
                                         ACT.Copy).then_inc(job_act, 1)

            def unit(b, un):
                kind, t = un
                if kind == "a":
                    return
                bank = banks[bank_of(b, un)]
                wide = bank[:, :].rearrange("p (k n) -> p k n", k=4)
                cols = slice(t * P, (t + 1) * P)
                if kind == "s":
                    if un == ("s", 0) and not (isinstance(b, int) and b <= 0):
                        act.wait_ge(y_added, 4 * b)
                    act.wait_ge(unit_dve, n_dve(b, un))
                    nc.scalar.activation(pbuf[:, t, :], bank[:, 0:S], ACT.Exp, bias=nmax[:, t:t + 1], scale=SM,
                                         accum_out=rowsum[:, t:t + 1]).then_inc(unit_act, 1)
                    return
                act.wait_ge(unit_full, n_full(b, un))
                if kind == "x":
                    if isinstance(b, int) and b == 0 and t == 0:
                        act.wait_ge(tern_made, PIECES)
                    nc.scalar.activation(xnT[:, HI, :, cols], wide, ACT.Copy).then_inc(unit_act, 1)
                elif kind == "L":
                    nc.scalar.activation(tstack[:, :], bank[:, :], ACT.Copy).then_inc(unit_act, 1)
                elif kind == "n1T":
                    nc.scalar.activation(n1T[:, HI, :, cols], wide, ACT.Copy).then_inc(unit_act, 1)
                elif kind == "n2T":
                    nc.scalar.activation(n2T[:, HI, :, cols], wide[:, 0:KC, :], ACT.Copy).then_inc(unit_act, 1)
                elif kind == "t":
                    nc.scalar.activation(tT[:, HI, t, :], bank[:, :], ACT.Identity, bias=tbias[:, t:t + 1]
                                         ).then_inc(unit_act, 1)
                elif kind == "v":
                    nc.scalar.activation(vo[:, HI, t, :], bank[:, :], ACT.Copy).then_inc(unit_act, 1)
                elif kind == "pT":
                    nc.scalar.activation(pT[:, HI, t, :, :], bank[:, :].rearrange("p (j q) -> p j q", j=2),
                                         ACT.Copy).then_inc(unit_act, 1)

            def steps(b, todo, odd=None):
                for st in todo:
                    if isinstance(st, str):
                        continue
                    kind, j = st
                    if kind in ("x", "L", "n1T", "n2T", "t", "s", "v", "pT", "a"):
                        unit(b, st)
                    elif kind == "up":
                        act.wait_ge(up_full, NFF * b + j + 1)
                        if not (isinstance(b, int) and b == 0 and j < 2):
                            act.wait_ge(sqlo_made, NFF * b + j - 1)
                        nc.scalar.activation(rbuf[:, j % 2, :], banks[f"H{j % 2}"][:, :], ACT.Relu,
                                             scale=scf[:, j:j + 1]).then_inc(relu_made, 1)
                    elif kind == "hi":
                        act.wait_ge(square_made, NFF * b + j + 1)
                        if not (isinstance(b, int) and b == 0 and j < 2):
                            act.wait_ge(down_full, NFF * b + j - 1)
                        nc.scalar.activation(qbuf[:, j % 2, HI, :], rbuf[:, j % 2, :], ACT.Copy
                                             ).then_inc(sqhi_made, 1)
                    elif kind == "abs":
                        act.wait_ge(ring_in[j % 2], 16 * (j // 2 + 1))
                        for i in range(4):
                            if 4 * j + i >= 2:
                                act.wait_ge(abs_done, 4 * j + i - 1)
                            nc.scalar.activation(absj[:, i % 2, :], wring[:, j % 2, i, :], ACT.Abs,
                                                 accum_out=asum[:, j, i:i + 1]).then_inc(abs_done, 1)
                    elif kind == "piece":
                        act.wait_ge(tern_turned, j + 1)
                        ps = banks[f"O{j % 4}"][:, 0:256].bitcast(BF16).rearrange("p (k n) -> p k n", k=4)
                        if j < NFF:
                            dst = fcT[:, :, j * P:(j + 1) * P]
                        else:
                            t, q = (j - NFF) // 4, (j - NFF) % 4
                            dst = projT[:, 4 * q:4 * q + 4, t * P:(t + 1) * P]
                        nc.scalar.activation(dst, ps, ACT.Copy).then_inc(tern_stored, 1)
                    elif kind == "ut":
                        act.wait_ge(ut_full, j + 1)
                        nc.scalar.activation(uT[:, j * 512:(j + 1) * 512], banks[f"H{j % 2}"][:, :], ACT.Copy
                                             ).then_inc(ut_stored, 1)
            run_bodies(act, steps)

        @block.vector
        def _(dve):
            OWN_PRO, OWN_BODY = [None], [None]
            chain = {"base": 0, "n": 0}

            def link(ins):
                chain["n"] += 1
                ins.then_inc(own, 1)
                dve.wait_ge(own, chain["base"] + chain["n"])

            def link_to_aggr(ins):
                link(ins)
                nc.vector.memset(spare[:, :], 0.0)

            for n, (kind, c) in enumerate(JOBS):
                if "dve" not in job_engines(n):
                    continue
                bank = banks[JBANK[n % 6]]
                if n == 1:
                    pass
                dve.wait_ge(job_full, n + 1)
                wide = bank[:, :].rearrange("p (k n) -> p k n", k=KE)
                if kind == "wqT":
                    nc.vector.tensor_copy(WqT[:, :, c * P:(c + 1) * P], wide).then_inc(job_dve, 1)
                elif kind == "wkT":
                    nc.vector.tensor_copy(WkT[:, :, c * P:(c + 1) * P], wide).then_inc(job_dve, 1)
                elif kind == "wvT":
                    nc.vector.tensor_copy(WvT[:, :, c * P:(c + 1) * P], wide).then_inc(job_dve, 1)
                elif kind == "bq":
                    nc.vector.tensor_tensor(bqp[:, :], bank[:, 0:KE], bqc[:, :], ALU.add).then_inc(job_dve, 1)
                elif kind == "bv":
                    dve.wait_ge(const_ready, 2)
                    link(nc.vector.tensor_tensor(bvp[:, :], bank[:, 0:KE], bvc[:, :], ALU.add))
                    for k in range(KE):
                        last = nc.vector.tensor_scalar(bvrep[:, k, :], ones[:, :], bvp[:, k:k + 1], None, ALU.mult)
                    last.then_inc(job_dve, 1)
                elif kind == "M":
                    dve.wait_ge(job_act, job_count(n, "act"))
                    nc.vector.scalar_tensor_tensor(out=M[:, LO, c, :], in0=bank[:, 0:DC], scalar=g1c[:, c:c + 1],
                                                   in1=M[:, HI, c, :], op0=ALU.mult, op1=ALU.subtract
                                                   ).then_inc(job_dve, 1)
                elif kind == "tb":
                    nc.vector.tensor_copy(tbias[:, :], bank[:, 0:KC]).then_inc(job_dve, 1)
                elif kind == "wvo":
                    dve.wait_ge(job_act, job_count(n, "act"))
                    nc.vector.scalar_tensor_tensor(out=Wvo[:, LO, c, :], in0=bank[:, :], scalar=g2c[:, c:c + 1],
                                                   in1=Wvo[:, HI, c, :], op0=ALU.mult, op1=ALU.subtract
                                                   ).then_inc(job_dve, 1)
                elif kind == "co":
                    nc.vector.tensor_tensor(crow[:, :], bank[:, :], borow, ALU.add).then_inc(job_dve, 1)
                elif kind == "fb":
                    dve.wait_ge(job_act, job_count(n, "act"))
                    nc.vector.tensor_tensor(FB[:, :, 64:128], bank[:, 0:KD * 64].rearrange("p (k n) -> p k n", k=KD),
                                            FB[:, :, 0:64], ALU.subtract).then_inc(job_dve, 1)
                if n == 3:
                    dve.wait_ge(params_in, 16 * 14)
                    dve.wait_ge(wk_in, 16)
                    for k in range(KC):
                        last = nc.vector.tensor_scalar(Wk_s[:, k, :], Wk_s[:, k, :], g2c[:, k:k + 1], None, ALU.mult)
                    last.then_inc(scales_made, 1)

            def unit(b, un):
                kind, t = un
                bank = banks[bank_of(b, un)]
                wide = bank[:, :].rearrange("p (k n) -> p k n", k=4)
                cols = slice(t * P, (t + 1) * P)
                if kind == "s":
                    dve.wait_ge(unit_full, n_full(b, un))
                    link(nc.vector.tensor_reduce(rowmax[:, t:t + 1], bank[:, 0:S], AX_X, ALU.max))
                    nc.vector.tensor_scalar(nmax[:, t:t + 1], rowmax[:, t:t + 1], -SM, None, ALU.mult
                                            ).then_inc(unit_dve, 1)
                    return
                if kind == "a":
                    dve.wait_ge(unit_full, n_full(b, un))
                    dve.wait_ge(res_made, 4 * (b + 1) + t + 1)
                    here = x2[cur["par"]]
                    nc.vector.scalar_tensor_tensor(out=here[:, t, :], in0=bank[:, :], scalar=rinv[:, t:t + 1],
                                                   in1=here[:, t, :], op0=ALU.mult, op1=ALU.add
                                                   ).then_inc(unit_dve, 1)
                    dve.wait_ge(unit_dve, n_dve(b, un))
                    link_to_aggr(nc.vector.bn_stats(nst[:, t, :], here[:, t, :]))
                    link(nc.vector.bn_aggr(nmv[:, t, :], nst[:, t, :]))
                    nc.vector.tensor_scalar(nrs[:, t:t + 1], nmv[:, t, 1:2], EPS, None, ALU.add).then_inc(var_made, 1)
                    return
                dve.wait_ge(unit_act, n_act(b, un))
                if kind == "x":
                    nc.vector.tensor_tensor(xnT[:, LO, :, cols], wide, xnT[:, HI, :, cols], ALU.subtract
                                            ).then_inc(unit_dve, 1)
                elif kind == "L":
                    nc.vector.tensor_tensor(tstack[32:64, :], bank[32:64, :], tstack[32:64, :], ALU.subtract)
                    nc.vector.tensor_tensor(tstack[96:128, :], bank[96:128, :], tstack[96:128, :], ALU.subtract
                                            ).then_inc(unit_dve, 1)
                elif kind == "n1T":
                    nc.vector.tensor_tensor(n1T[:, LO, :, cols], wide, n1T[:, HI, :, cols], ALU.subtract
                                            ).then_inc(unit_dve, 1)
                elif kind == "n2T":
                    nc.vector.tensor_tensor(n2T[:, LO, :, cols], wide[:, 0:KC, :], n2T[:, HI, :, cols], ALU.subtract
                                            ).then_inc(unit_dve, 1)
                elif kind == "t":
                    nc.vector.scalar_tensor_tensor(out=tT[:, LO, t, :], in0=bank[:, :], scalar=tbias[:, t:t + 1],
                                                   in1=tT[:, HI, t, :], op0=ALU.add, op1=ALU.subtract
                                                   ).then_inc(unit_dve, 1)
                elif kind == "v":
                    nc.vector.tensor_tensor(vo[:, LO, t, :], bank[:, :], vo[:, HI, t, :], ALU.subtract
                                            ).then_inc(unit_dve, 1)
                elif kind == "pT":
                    nc.vector.tensor_tensor(pT[:, LO, t, :, :], bank[:, :].rearrange("p (j q) -> p j q", j=2),
                                            pT[:, HI, t, :, :], ALU.subtract).then_inc(unit_dve, 1)
                    link(nc.vector.reciprocal(rinv[:, 2 * t:2 * t + 2], rowsum[:, 2 * t:2 * t + 2]))

            cur = {"par": 0}

            def evacuate(g, t):
                if t == 0:
                    dve.wait_ge(down_full, NFF * (g + 1))
                if t >= 2 or (isinstance(g, int) and g == NG - 1):
                    dve.wait_ge(y_added, 4 * g + t - 1)
                nc.vector.tensor_tensor(yb[:, t % 2, :], banks[f"O{t}"][:, :], sprow[:, :], ALU.mult
                                        ).then_inc(y_made, 1)

            def steps(b, todo, odd=None):
                first = isinstance(b, int) and b < 0
                g = b + 1
                cur["par"] = 0 if first else (odd + 1) % 2 if odd is not None else (b + 1) % 2
                prev = 1 - cur["par"]
                if first:
                    chain["base"] = 0
                    chain["pro"] = None
                else:
                    if chain["pro"] is None:
                        chain["pro"] = chain["n"]
                    chain["base"] = chain["pro"] + PER_BODY * b
                    chain["n"] = 0
                for st in todo:
                    kind, j = st if isinstance(st, tuple) else (st, None)
                    if kind in ("x", "L", "n1T", "n2T", "t", "s", "v", "pT", "a"):
                        unit(b, st)
                    elif kind == "xstats":
                        dve.wait_ge(x_in_s, 16 * (g + 1))
                        for t in range(TILES):
                            last = nc.vector.bn_stats(xst[:, t, :], xb[:, t, :])
                        link_to_aggr(last)
                        for t in range(TILES):
                            last = nc.vector.bn_aggr(xmv[:, t, :], xst[:, t, :])
                        link(last)
                        nc.vector.tensor_scalar(xrs[:, :], xmv[:, :, 1], 1.0 + EPS, EPS * EPS, ALU.mult, ALU.add
                                                ).then_inc(var_made, 1)
                    elif kind == "cstats":
                        dve.wait_ge(ctx_in_s, 16 * (g + 1))
                        for t in range(TILES):
                            last = nc.vector.bn_stats(cst[:, t, :], ctxb[:, t, :])
                        link_to_aggr(last)
                        for t in range(TILES):
                            last = nc.vector.bn_aggr(cmv[:, t, :], cst[:, t, :])
                        link(last)
                        nc.vector.tensor_scalar(crs[:, :], cmv[:, :, 1], EPS, None, ALU.add).then_inc(var_made, 1)
                    elif kind[:2] == "nx":
                        t = int(kind[2])
                        if t >= 2:
                            dve.wait_ge(unit_full, n_full(b, ("n1T", t - 2)))
                        elif not first:
                            dve.wait_ge(unit_full, n_full(b, ("x", t + 2)))
                        if t == 0:
                            dve.wait_ge(rstd_made, NROOT * g + 1)
                        nc.vector.tensor_scalar(nrm[:, t % 2, :], xb[:, t, :], xmv[:, t, 0:1], xrs[:, t:t + 1],
                                                ALU.subtract, ALU.mult).then_inc(n1_made, 1)
                    elif kind[:2] == "nc":
                        t = int(kind[2])
                        if t == 0:
                            dve.wait_ge(rstd_made, NROOT * g + 2)
                        nc.vector.tensor_scalar(ctxb[:, t, :], ctxb[:, t, :], cmv[:, t, 0:1], crs[:, t:t + 1],
                                                ALU.subtract, ALU.mult).then_inc(n2_made, 1)
                    elif kind[:2] == "nX":
                        t = int(kind[2])
                        here = cur["par"] if t < 2 else prev
                        dve.wait_ge(rstd_made, NROOT * (g if t < 2 else b) + 3 + t)
                        if t >= 2:
                            dve.wait_ge(unit_full, n_full(b, ("x", t - 2)))
                        nc.vector.tensor_scalar(nrm[:, t % 2, :], x2[here][:, t, :], nmv[:, t, 0:1], nrs[:, t:t + 1],
                                                ALU.subtract, ALU.mult).then_inc(xn_made, 1)
                    elif kind == "out":
                        for t in range(TILES):
                            evacuate(b - 1, t)
                    elif kind == "sq":
                        dve.wait_ge(relu_made, NFF * b + j + 1)
                        nc.vector.tensor_tensor(rbuf[:, j % 2, :], rbuf[:, j % 2, :], rbuf[:, j % 2, :], ALU.mult
                                                ).then_inc(square_made, 1)
                    elif kind == "lo":
                        dve.wait_ge(sqhi_made, NFF * b + j + 1)
                        nc.vector.tensor_tensor(qbuf[:, j % 2, LO, :], rbuf[:, j % 2, :], qbuf[:, j % 2, HI, :],
                                                ALU.subtract).then_inc(sqlo_made, 1)
                    elif kind == "scale":
                        dve.wait_ge(abs_done, 4 * j + 4)
                        if j < 4:
                            sc, n = scf[:, 4 * j:4 * j + 4], 4
                            link(nc.vector.tensor_scalar(sc, asum[:, j, :], 1.0 / D, EPS, ALU.mult, ALU.max))
                        else:
                            sc, n = spc[:, j - 4:j - 3], 1
                            link(nc.vector.tensor_reduce(psum4[:, j - 4:j - 3], asum[:, j, :], AX_X, ALU.add))
                            link(nc.vector.tensor_scalar(sc, psum4[:, j - 4:j - 3], 1.0 / HID, EPS, ALU.mult, ALU.max))
                        link(nc.vector.tensor_scalar(half[:, j % 2, 0:n], sc, 0.5, None, ALU.mult))
                        link(nc.vector.tensor_scalar(nhalf[:, j % 2, 0:n], sc, -0.5, None, ALU.mult))
                    elif kind == "piece":
                        gr, i = j // 4, j % 4
                        at = i if gr < 4 else 0
                        w = wring[:, gr % 2, i, :]
                        if j >= 4:
                            dve.wait_ge(tern_turned, j - 3)
                        if j >= 2:
                            dve.wait_ge(tern_made, j - 1)
                        link(nc.vector.tensor_scalar(below[:, j % 2, :], w, nhalf[:, gr % 2, at:at + 1], None, ALU.is_lt))
                        nc.vector.scalar_tensor_tensor(out=tern[:, i, :], in0=w, scalar=half[:, gr % 2, at:at + 1],
                                                       in1=below[:, j % 2, :], op0=ALU.is_gt, op1=ALU.subtract
                                                       ).then_inc(tern_made, 1)
                    elif kind == "uprep":
                        link(nc.vector.reciprocal(urs[:, :], scf[:, :]))
                        link(nc.vector.tensor_scalar(urs[:, :], urs[:, :], gatec[:, 0:1], None, ALU.mult))
                        link(nc.vector.tensor_tensor(u_s[:, :, :], u_s[:, :, :],
                                                     urs[:, :].unsqueeze(2).broadcast_to([P, NFF, RK]), ALU.mult))
                        link(nc.vector.tensor_copy(uhi[:, :, :], u_s[:, :, :]))
                        for i in range(4):
                            nc.vector.tensor_copy(unat[:, :, 2 * i, :], uhi[:, :, :])
                            last = nc.vector.tensor_tensor(unat[:, :, 2 * i + 1, :], u_s[:, :, :], uhi[:, :, :],
                                                           ALU.subtract)
                        last.then_inc(unat_made, 1)
                    elif kind == "sprow":
                        dve.wait_ge(ut_full, 4)
                        for t in range(KD):
                            last = nc.vector.tensor_scalar(bvrep[:, t, :], ident[:, :], spc[:, t:t + 1], None, ALU.mult)
                        last.then_inc(diag_made, 1)
                        dve.wait_ge(sprow_full, 1)
                        link(nc.vector.tensor_copy(sprow[:, :], banks["H0"][:, :]))
                if not first and not (isinstance(b, int) and b == NG - 1):
                    assert chain["n"] == PER_BODY, chain["n"]

            PER_BODY = 2 + 2 + 4 + 8 + 2
            run_bodies(dve, steps)
            for t in range(TILES):
                evacuate(NG - 1, t)

        @block.tensor
        def _(pe):
            pe.wait_ge(const_ready, 2)
            for n, (kind, c) in enumerate(JOBS):
                bank = banks[JBANK[n % 6]]
                if n >= 6:
                    job_read(pe, n - 6)
                if kind in ("wqT", "wkT", "wvT"):
                    if kind == "wqT":
                        pe.wait_ge(wq_in, 16)
                    elif kind == "wkT":
                        pe.wait_ge(scales_made, 1)
                    else:
                        pe.wait_ge(wv_in, 16)
                    w = {"wqT": Wq_s, "wkT": Wk_s, "wvT": Wv_s}[kind]
                    for k in range(KE):
                        mm = pe.transpose(bank[:, k * P:(k + 1) * P], w[:, c, k * P:(k + 1) * P], ident[:, :])
                elif kind == "bq":
                    pe.wait_ge(params_in, 16 * 14)
                    for e in range(KE):
                        for k in range(KD):
                            mm = pe.matmul(bank[:, e:e + 1], Wq_s[:, k, e * P:(e + 1) * P], b1c[:, k:k + 1],
                                           start=(k == 0), stop=(k == KD - 1))
                elif kind == "bv":
                    for e in range(KE):
                        for k in range(KC):
                            mm = pe.matmul(bank[:, e:e + 1], Wv_s[:, k, e * P:(e + 1) * P], b2c[:, k:k + 1],
                                           start=(k == 0), stop=(k == KC - 1))
                elif kind == "M":
                    if c == 0:
                        for last in (KD + KC - 2, KD + KC - 1):
                            job_read(pe, last)
                    for k in range(KE):
                        mm = pe.matmul(bank[:, 0:DC], WqT[:, k, c * P:(c + 1) * P], WkT[:, k, :],
                                       start=(k == 0), stop=(k == KE - 1))
                elif kind == "tb":
                    job_read(pe, JOBS.index(("bq", 0)))
                    for m in range(KC):
                        for k in range(KE):
                            mm = pe.matmul(bank[:, m:m + 1], WkT[:, k, m * P:(m + 1) * P], bqp[:, k:k + 1],
                                           start=(k == 0), stop=(k == KE - 1))
                elif kind == "wvo":
                    if c == 0:
                        pe.wait_ge(wo_in, 16)
                        for last in (JOBS.index(("wvT", KC - 2)), JOBS.index(("wvT", KC - 1))):
                            job_read(pe, last)
                    for k in range(KE):
                        mm = pe.matmul(bank[:, :], WvT[:, k, c * P:(c + 1) * P], Wo_s[:, k, :],
                                       start=(k == 0), stop=(k == KE - 1))
                elif kind == "co":
                    job_read(pe, JOBS.index(("bv", 0)))
                    for k in range(KE):
                        mm = pe.matmul(bank[:, :], bvrep[:, k, :], Wo_s[:, k, :], start=(k == 0), stop=(k == KE - 1))
                elif kind == "fb":
                    for k in range(KD):
                        mm = pe.matmul(bank[:, k * 64:(k + 1) * 64], v_s[:, k * P:(k + 1) * P],
                                       fbT4[:, :, :].rearrange("s i r -> s (i r)"), start=True, stop=True)
                mm.then_inc(job_full, 1)
            pe.wait_ge(job_dve, job_count(len(JOBS) - 1, "dve"))

            def products(bank, pairs):
                for i, (w, m) in enumerate(pairs):
                    mm = pe.matmul(bank, w, m, start=(i == 0), stop=(i == len(pairs) - 1))
                return mm

            THREE = [(HI, HI), (HI, LO), (LO, HI)]

            def unit(b, un):
                kind, t = un
                name = bank_of(b, un)
                bank = banks[name]
                before = bank_before(b, un)
                cols = slice(t * P, (t + 1) * P)
                if un in (("x", 2), ("x", 3)):
                    if isinstance(b, int) and b == 0:
                        pe.wait_ge(tern_stored, PIECES)
                        pe.wait_ge(own, sprow_read[0])
                    else:
                        pe.wait_ge(relu_made, NFF * (b - 1) + NFF - 1 + (t == 3))
                elif before:
                    if before[1][0] == "s":
                        pe.wait_ge(unit_act, n_act(*before))
                    else:
                        pe.wait_ge(unit_dve, n_dve(*before))
                if kind in ("x", "n1T", "n2T"):
                    src, made = {"x": (nrm[:, t % 2, :], xn_made), "n1T": (nrm[:, t % 2, :], n1_made),
                                 "n2T": (ctxb[:, t, :], n2_made)}[kind]
                    pe.wait_ge(made, 4 * (b if kind == "x" else b + 1) + t + 1)
                    for k in range(KC if kind == "n2T" else KD):
                        mm = pe.transpose(bank[:, k * P:(k + 1) * P], src[:, k * P:(k + 1) * P], ident[:, :])
                elif kind == "L":
                    pe.wait_ge(unit_dve, n_dve(b, ("x", 3)))
                    mm = products(bank[:, :], [(FB[:, k, :], xnT[:, h, k, :]) for k in range(KD) for h in (HI, LO)])
                elif kind == "t":
                    pe.wait_ge(unit_dve, n_dve(b, ("n1T", 3)))
                    mm = products(bank[:, :], [(M[:, w, k, cols], n1T[:, m, k, :]) for k in range(KD) for w, m in THREE])
                elif kind == "s":
                    c = t // 2
                    if t == 0:
                        pe.wait_ge(unit_dve, n_dve(b, ("t", 2)))
                    mm = products(bank[:, 0:S], [(tT[:, w, k, cols], n2T[:, m, k, c * S:(c + 1) * S])
                                                 for k in range(KC) for w, m in THREE])
                elif kind == "v":
                    mm = products(bank[:, :], [(n2T[:, w, k, cols], Wvo[:, m, k, :]) for k in range(KC)
                                               for w, m in THREE])
                elif kind == "pT":
                    pe.wait_ge(unit_act, n_act(b, ("s", 2 * t + 1)))
                    for j in range(2):
                        for q in range(2):
                            mm = pe.transpose(bank[:, j * S + q * P:j * S + (q + 1) * P],
                                              pbuf[:, 2 * t + q, j * P:(j + 1) * P], ident[:, :])
                elif kind == "a":
                    c, q = t // 2, t % 2
                    pe.wait_ge(unit_dve, max(n_dve(-1, ("v", 2 * c + 1)), n_dve(-1, ("pT", c)))
                               if isinstance(b, int) and b < 0 else n_dve(b, ("pT", c)))
                    mm = products(bank[:, :], [(pT[:, w, c, j, q * P:(q + 1) * P], vo[:, m, 2 * c + j, :])
                                               for j in range(2) for w, m in THREE])
                mm.then_inc(unit_full, 1)

            def down(b, j):
                pe.wait_ge(sqlo_made, NFF * b + j + 1)
                if j == 0:
                    if isinstance(b, int) and b == 0:
                        pe.wait_ge(tern_stored, PIECES)
                    else:
                        pe.wait_ge(y_made, 4 * b)
                for t in range(TILES):
                    for h in (HI, LO):
                        mm = pe.matmul(banks[f"O{t}"][:, :], qbuf[:, j % 2, h, t * P:(t + 1) * P], projT[:, j, :],
                                       start=(j == 0 and h == HI), stop=(j == NFF - 1 and h == LO))
                mm.then_inc(down_full, 1)

            def steps(b, todo, odd=None):
                for st in todo:
                    kind, j = st if isinstance(st, tuple) else (st, None)
                    if kind in ("x", "L", "n1T", "n2T", "t", "s", "v", "pT", "a"):
                        unit(b, st)
                    elif kind == "up":
                        if j == 0:
                            pe.wait_ge(unit_dve, n_dve(b, ("x", 3)))
                        elif j >= 2:
                            pe.wait_ge(relu_made, NFF * b + j - 1)
                        for k in range(KD):
                            for h in (HI, LO):
                                pe.matmul(banks[f"H{j % 2}"][:, :], fcT[:, k, j * P:(j + 1) * P], xnT[:, h, k, :],
                                          start=(k == 0 and h == HI), stop=False)
                        if j == 0:
                            pe.wait_ge(unit_dve, n_dve(b, ("L", 0)))
                            if isinstance(b, int) and b == 0:
                                pe.wait_ge(ut_stored, 4)
                        pe.matmul(banks[f"H{j % 2}"][:, :], uT[:, j * P:(j + 1) * P], tstack[:, :],
                                  start=False, stop=True).then_inc(up_full, 1)
                    elif kind == "down":
                        down(b, j)
                    elif kind == "down-":
                        down(b - 1, j)
                    elif kind == "piece":
                        pe.wait_ge(tern_made, j + 1)
                        if j >= 4:
                            pe.wait_ge(tern_stored, j - 3)
                        ps = banks[f"O{j % 4}"][:, 0:256].bitcast(BF16)
                        for k in range(4):
                            mm = pe.transpose(ps[:, k * P:(k + 1) * P], tern[:, j % 4, k * P:(k + 1) * P], identb[:, :])
                        mm.then_inc(tern_turned, 1)
                    elif kind == "ut":
                        if j == 0:
                            pe.wait_ge(unat_made, 1)
                        if j >= 2:
                            pe.wait_ge(ut_stored, j - 1)
                        for i in range(4):
                            mm = pe.transpose(banks[f"H{j % 2}"][:, i * P:(i + 1) * P],
                                              unat[:, 4 * j + i, :, :].rearrange("p i r -> p (i r)"), ident[:, :])
                        mm.then_inc(ut_full, 1)
                    elif kind == "sprow":
                        pe.wait_ge(ut_stored, 4)
                        pe.wait_ge(diag_made, 1)
                        for t in range(KD):
                            mm = pe.matmul(banks["H0"][:, t * P:(t + 1) * P], ones[:, :], bvrep[:, t, :],
                                           start=True, stop=True)
                        mm.then_inc(sprow_full, 1)

            sprow_read = [1 + (2 + 2 + 4 + 8 + 2) + 4 * 3 + 4 * 4 + 32 + 4 + 1]
            run_bodies(pe, steps)
            for j in (NFF - 2, NFF - 1):
                down(NG - 1, j)


_INS = ['x', 'ctx_768', 'L0_xattn_ln1_g', 'L0_xattn_ln1_b', 'L0_xattn_ln2_g', 'L0_xattn_ln2_b', 'L0_xattn_Wq',
        'L0_xattn_bq', 'L0_xattn_Wk', 'L0_xattn_bk', 'L0_xattn_Wv', 'L0_xattn_bv', 'L0_xattn_Wo', 'L0_xattn_bo',
        'L0_ffn_fast_b', 'L0_ffn_w_fc', 'L0_ffn_w_proj', 'L0_ffn_u', 'L0_ffn_v', 'L0_ffn_gate']
_OUTS = [((16, 256, 512), 'float32')]


def kernel(**inputs):
    import numpy as _np
    import concourse.bacc as _bacc
    from concourse import mybir as _mybir
    from concourse.bass_utils import run_bass_kernel_spmd as _run

    nc = _bacc.Bacc("TRN2", target_bir_lowering=False, num_devices=1, dynamic_dma_scratch_size=1024)
    arrays, args = {}, []
    for name in _INS:
        a = _np.ascontiguousarray(inputs[name])
        arrays[f"in_{name}_dram"] = a
        args.append(nc.dram_tensor(f"in_{name}_dram", a.shape, _mybir.dt.from_np(a.dtype), kind="ExternalInput").ap())
    for i, (shape, dtype) in enumerate(_OUTS):
        dt = _mybir.dt.from_np(_np.dtype(dtype))
        args.append(nc.dram_tensor(f"out_{i}_dram", shape, dt, kind="ExternalOutput").ap())
    mk_xattn_ffn(nc, *args)
    r = _run(nc, [arrays], core_ids=[0])
    got = tuple(r.results[0][f"out_{i}_dram"] for i in range(len(_OUTS)))
    return got[0]
```

```python
from contextlib import ExitStack

import concourse.bass as bass
from concourse import mybir

P = 128
ALU = mybir.AluOpType
ACT = mybir.ActivationFunctionType
F32 = mybir.dt.float32
F32R = mybir.dt.float32r
BF16 = mybir.dt.bfloat16
AX_X = mybir.AxisListType.X
HI, LO = 0, 1
EPS = 1e-5

TILES = 4
TOK = TILES * P
NPRE = 25
NBODY = 30
NROOT = 6
NFF = 16
PIECES = 2 * NFF
TAIL = 4

ATTENTION = ([("n1T", t) for t in range(4)] + [("n2T", t) for t in range(4)]
             + [("t", 0), ("t", 1), ("t", 2), ("s", 0), ("s", 1), ("v", 0), ("v", 1), ("pT", 0),
                ("s", 2), ("a", 0), ("s", 3), ("a", 1), ("v", 2), ("v", 3), ("pT", 1), ("a", 2), ("a", 3)])
BODY = [("x", 0), ("x", 1), ("x", 2), ("x", 3), ("L", 0)] + ATTENTION
assert len(ATTENTION) == NPRE and len(BODY) == NBODY


def unit_list(b):
    return ATTENTION if isinstance(b, int) and b < 0 else BODY


def units_before(b, kept):
    if isinstance(b, int) and b < 0:
        return 0
    return b * sum(map(kept, BODY)) + sum(map(kept, ATTENTION))


def count(b, unit, kept=lambda u: True):
    seq = unit_list(b)
    return units_before(b, kept) + sum(map(kept, seq[:seq.index(unit) + 1]))


def on_act(unit):
    return unit[0] != "a"


def n_full(b, unit):
    return count(b, unit)


def n_act(b, unit):
    return count(b, unit, on_act)


def n_dve(b, unit):
    return count(b, unit)


def bank_of(b, unit):
    if unit == ("x", 2):
        return "H0"
    if unit == ("x", 3):
        return "H1"
    n = unit_list(b).index(unit)
    if unit_list(b) is ATTENTION and n >= 8:
        return ("G0", "H0", "G1", "H1")[n % 4]
    return f"G{n % 2}"


def bank_before(b, unit):
    seq, bank = unit_list(b), bank_of(b, unit)
    for u in reversed(seq[:seq.index(unit)]):
        if bank_of(b, u) == bank:
            return b, u
    if isinstance(b, int) and b < 0:
        return None
    for u in reversed(unit_list(b - 1)):
        if bank_of(b - 1, u) == bank:
            return b - 1, u


PLACED = {
    3: ["xs01"], 4: ["xs23"], 5: ["cs01"], 6: ["nx0", "cs23"], 7: ["nx1", ("n1T", 0), "nc0"],
    8: [("n1T", 1), "nx2", "nc1"], 9: [("n1T", 2), "nx3", "nc2"], 10: [("n1T", 3), "nc3"], 11: [("n2T", 0)],
    12: [("n2T", 1), ("n2T", 2)], 13: [("n2T", 3), "residual"],
    14: [("t", 0)], 15: [("t", 1)], 16: [("t", 2)], 18: [("s", 0)], 19: [("s", 1)], 20: [("v", 0)],
    21: [("v", 1), ("pT", 0)], 22: [("s", 2)], 23: [("a", 0), "nX0"], 24: [("s", 3)], 25: [("a", 1), "nX1"],
    26: [("v", 2)], 27: [("v", 3)], 28: [("pT", 1)], 29: [("a", 2)], 30: [("a", 3)],
}
assert [s for h in sorted(PLACED) for s in PLACED[h] if isinstance(s, tuple)] == ATTENTION


def body_steps(attention, leftover):
    out = [("x", 0), "nX2", ("x", 1), "nX3"]
    if leftover:
        out += [("down-", NFF - 2)]
    out += [("x", 2), ("x", 3)]
    if leftover:
        out += [("down-", NFF - 1), "out01"]
    out += [("L", 0)]
    if leftover:
        out += ["out23"]
    for j in range(NFF):
        out += [("up", j)]
        out += PLACED.get(2 * j, []) if attention else []
        out += [("sq", j), ("hi", j)]
        if j >= 2:
            out += [("down", j - 2)]
        out += PLACED.get(2 * j + 1, []) if attention else []
        out += [("lo", j)]
    return out


def piece_steps():
    out = [("abs", k) for k in range(4)] + [("scale", 0), ("sign", 0)] + [("abs", k) for k in (4, 5)]
    for j in range(PIECES + 3):
        if j % 4 == 3 and j // 4 + 1 < 8:
            out += [("scale", j // 4 + 1)]
        if j + 1 < PIECES:
            out += [("sign", j + 1)]
        if j < PIECES:
            out += [("tern", j)]
        if 1 <= j <= PIECES:
            out += [("turn", j - 1)]
        if j >= 3:
            out += [("store", j - 3)]
        if j < 2 or 3 <= j <= PIECES - 6:
            out += [("abs", j + 6 if j < 2 else j + 5)]
        if j == 18:
            out += ["uprep"]
        if j in (22, 23, 24, 25):
            out += [("ut", j - 22)]
        if j == 30:
            out += ["diag"]
        if j == 32:
            out += ["sprow"]
        if j == 34:
            out += ["sprow_out"]
    return out


def prologue_steps(engine):
    def jobs(kind, n=1):
        return [("job", JOBS.index((kind, c))) for c in range(n)]

    wq, wk, wv, M, wvo = jobs("wqT", 4), jobs("wkT", 3), jobs("wvT", 3), jobs("M", 4), jobs("wvo", 3)
    head = [wq[0], wq[1], wq[2], wq[3], "gainK"]
    blocks = [(1, [wk[0]]), (1, [wk[1], "xs01"]), (1, [wk[2], "xs23"]), (1, jobs("bq")),
              (3, [M[0], "nx0", "nx1"]), (3, [M[1], "cs01", "cs23"]),
              (3, [M[2], "nc0", "nc1"]), (3, [M[3], "nc2", "nc3"]), (1, jobs("tb")),
              (1, [("n1T", 0), "nx2"]), (1, [wv[0]]), (1, [("n1T", 1), "nx3"]), (1, [wv[1]]), (1, [("n1T", 2)]),
              (1, [wv[2]]), (1, [("n1T", 3)]), (1, jobs("bv")), (1, [("n2T", 0)]), (3, [wvo[0]]),
              (1, [("n2T", 1)]), (3, [wvo[1]]), (1, [("n2T", 2)]), (3, [wvo[2]]), (1, [("n2T", 3)]),
              (4, jobs("co")), (3, [("t", 0)]), (1, jobs("fb")), (3, [("t", 1)]), (3, [("t", 2)]),
              (1, [("s", 0)]), (1, [("s", 1)]), (2, [("v", 0), "residual"]), (2, [("v", 1)]), (1, [("pT", 0)]),
              (1, [("s", 2)]), (1, [("a", 0)]), (1, [("s", 3), "nX0"]), (1, [("a", 1)]), (2, [("v", 2), "nX1"]),
              (2, [("v", 3)]), (1, [("pT", 1)]), (1, [("a", 2)]), (1, [("a", 3)])]
    pieces = piece_steps()
    total = sum(w for w, _ in blocks) - TAIL
    out, done, weight = head, 0, 0
    for w, own in blocks:
        weight += w
        want = min(len(pieces), len(pieces) * weight // total)
        share = pieces[done:want]
        done = want
        if engine == "pe":
            out = out + own + share
        else:
            out = out + share + [s for s in own if isinstance(s, str)] + [s for s in own if not isinstance(s, str)]
    return out


JOBS = ([("wqT", c) for c in range(4)] + [("wkT", c) for c in range(3)] + [("bq", 0)]
        + [("M", c) for c in range(4)] + [("tb", 0)] + [("wvT", c) for c in range(3)] + [("bv", 0)]
        + [("wvo", c) for c in range(3)] + [("co", 0), ("fb", 0)])


def mk_xattn_ffn(nc, x, ctx_768, ln1_g, ln1_b, ln2_g, ln2_b, Wq, bq, Wk, bk, Wv, bv, Wo, bo,
                 fast_b, w_fc, w_proj, u, v, gate, out):
    NB, S, D = x.shape
    DC = ctx_768.shape[2]
    E = Wq.shape[1]
    HID = w_fc.shape[0]
    RK = fast_b.shape[0]
    KD, KC, KE = D // P, DC // P, E // P
    NG = NB * S // TOK
    assert S == 256 and D == 512 and E == 512 and HID == NFF * P and RK == 16 and NG == 8
    SM = float(E) ** -0.5

    x_in = x.rearrange("(g c) (p t) d -> g p c (t d)", c=2, t=2)
    ctx_in = ctx_768.rearrange("(g c) (p t) d -> g p c (t d)", c=2, t=2)
    out_v = out.rearrange("(g c) (p t) d -> g c p (t d)", c=2, t=2)

    with ExitStack() as stack:
        def sb(name, shape, dt=F32, where=stack):
            return where.enter_context(nc.sbuf_tensor(name, shape, dt))

        def sem(name):
            return stack.enter_context(nc.semaphore(name))

        fcT = sb("fcT", [P, KD, HID], F32R)
        projT = sb("projT", [P, NFF, D], F32R)
        M = sb("M", [P, 2, KD, DC], F32R)
        Wvo = sb("Wvo", [P, 2, KC, D], F32R)
        uT = sb("uT", [P, HID], F32R)
        FB = sb("FB", [P, KD, P], F32R)
        ident = sb("ident", [P, P])
        identb = sb("identb", [P, P], BF16)
        sprow = sb("sprow", [P, D])
        crow = sb("crow", [P, D])
        tbias = sb("tbias", [P, KC])
        scf = sb("scf", [P, NFF])
        half = sb("half", [P, 2, 4])
        spc = sb("spc", [P, KD])
        asum = sb("asum", [P, 8, 4])
        psum4 = sb("psum4", [P, 4])
        urs = sb("urs", [P, NFF])
        g1c = sb("g1c", [P, KD])
        b1c = sb("b1c", [P, KD])
        g2c = sb("g2c", [P, KC])
        b2c = sb("b2c", [P, KC])
        bqc = sb("bqc", [P, KE])
        bvc = sb("bvc", [P, KE])
        bqp = sb("bqp", [P, KE])
        bvp = sb("bvp", [P, KE])
        gatec = sb("gatec", [P, 1])
        xst = sb("xst", [P, TILES, 6])
        xmv = sb("xmv", [P, TILES, 2])
        xrs = sb("xrs", [P, TILES])
        cst = sb("cst", [P, TILES, 6])
        cmv = sb("cmv", [P, TILES, 2])
        crs = sb("crs", [P, TILES])
        mhalf = sb("mhalf", [P, TILES])
        spare = sb("spare", [P, 1])
        nst = sb("nst", [P, TILES, 6])
        nmv = sb("nmv", [P, TILES, 2])
        nrs = sb("nrs", [P, TILES])
        rowmax = sb("rowmax", [P, TILES])
        nmax = sb("nmax", [P, TILES])
        rowsum = sb("rowsum", [P, TILES])
        rinv = sb("rinv", [P, TILES])
        ctxb = sb("ctxb", [P, TILES, DC])
        xb = sb("xb", [P, TILES, D])
        pbuf = sb("pbuf", [P, TILES, S])
        nrm = sb("nrm", [P, 2, D])
        tstack = sb("tstack", [P, TOK], F32R)
        x2a = sb("x2a", [P, TILES, D])
        ybuf = [pbuf[:, 2 * t:2 * t + 2, :].rearrange("p a s -> p (a s)") for t in range(2)] + [
            nrm[:, t, :] for t in range(2)]

        setup = ExitStack()
        wring = sb("wring", [P, 2, 4, D], F32, setup)
        Wq_s = sb("Wq_s", [P, KD, E], F32, setup)
        Wk_s = sb("Wk_s", [P, KC, E], F32, setup)
        WqT = sb("WqT", [P, KE, D], F32, setup)
        WkT = sb("WkT", [P, KE, DC], F32, setup)
        Wv_s = sb("Wv_s", [P, KC, E], F32, setup)
        WvT = sb("WvT", [P, KE, DC], F32, setup)
        Wo_s = sb("Wo_s", [P, KE, D], F32, setup)
        tern = sb("tern", [P, 4, D], BF16, setup)
        unat = sb("unat", [P, NFF, 8, RK], F32, setup)
        ones = sb("ones", [P, P], F32, setup)
        bvrep = sb("bvrep", [P, KE, P], F32, setup)
        signs = sb("signs", [P, 2, D], BF16, setup)
        absj = sb("absj", [P, 2, D], BF16, setup)
        u_s = sb("u_s", [P, NFF, RK], F32, setup)
        fbT4 = sb("fbT4", [RK, 4, RK], F32, setup)
        borow_t = sb("borow", [P, D], F32, setup)
        borow = borow_t[:, :]
        uhi = sb("uhi", [P, NFF, RK], F32R, setup)
        setup.close()
        xnT = sb("xnT", [P, 2, KD, TOK], F32R)
        n1T = sb("n1T", [P, 2, KD, TOK], F32R)
        n2T = sb("n2T", [P, 2, KC, TOK], F32R)
        tT = sb("tT", [P, 2, KC, TOK], F32R)
        pT = sb("pT", [P, 2, 2, 2, S], F32R)
        rbuf = sb("rbuf", [P, 2, TOK])
        x2b = sb("x2b", [P, TILES, D])
        qbuf = sb("qbuf", [P, 2, 2, TOK], F32R)
        vo = n1T
        x2 = [x2a, x2b]
        v_s = pbuf[0:RK, 0:2, :].rearrange("p a b -> p (a b)")

        banks = {n: stack.enter_context(nc.psum_tensor(n, [P, 512], F32))
                 for n in ("G0", "G1", "H0", "H1", "O0", "O1", "O2", "O3")}

        gains_in, lowrank_in = sem("gains_in"), sem("lowrank_in")
        qbias_in, vbias_in = sem("q_biases_in"), sem("v_biases_in")
        gained = sem("Wk_gained")
        signs_made = sem("signs_made")
        sprow_made = sem("sprow_made")
        wq_in, wk_in, wv_in, wo_in = sem("wq_in"), sem("wk_in"), sem("wv_in"), sem("wo_in")
        x_in_s, ctx_in_s = sem("x_loaded"), sem("ctx_loaded")
        ring_in = [sem(f"ring{i}_in") for i in range(8)]
        stored = sem("stored")
        const_ready = sem("const_ready")
        job_full = sem("job_full")
        job_act = sem("job_act")
        job_dve = sem("job_dve")
        own = sem("dve_chain")
        pool_own = sem("pool_chain")
        abs_done = sem("abs_done")
        scales_made = sem("scales_made")
        tern_made = sem("tern_made")
        tern_turned = sem("tern_turned")
        even_stored, odd_stored = sem("even_pieces_stored"), sem("odd_pieces_stored")
        unat_made = sem("unat_made")
        ut_full = sem("ut_full")
        ut_stored = sem("ut_stored")
        diag_made = sem("diag_made")
        sprow_full = sem("sprow_full")
        unit_full = sem("unit_full")
        unit_act = sem("unit_act")
        unit_dve = sem("unit_dve")
        var_made = sem("var_made")
        rstd_made = sem("rstd_made")
        n1_made = sem("n1_made")
        n2_made = sem("n2_made")
        xn_made = sem("xn_made")
        res_made = sem("residual_made")
        up_full = sem("up_full")
        relu_made = sem("relu_made")
        square_made = sem("square_made")
        sqhi_made = sem("square_hi_made")
        sqlo_made = sem("square_lo_made")
        down_full = sem("down_full")
        y_made = sem("y_made")
        y_added = sem("y_added")

        def job_engines(n):
            kind = JOBS[n][0]
            if kind in ("wqT", "wkT", "wvT"):
                return ("act",) if n % 2 == 0 else ("dve",)
            return ("act", "dve") if kind in ("M", "wvo", "fb") else ("dve",)

        def job_count(n, engine):
            return sum(engine in job_engines(i) for i in range(n + 1))

        def job_read(e, n):
            last = job_engines(n)[-1]
            e.wait_ge(job_act if last == "act" else job_dve, job_count(n, last))

        def run_bodies(e, steps, engine=""):
            steps(-1, prologue_steps(engine))
            steps(0, body_steps(True, False))
            with e.Fori(0, (NG - 2) // 2) as pair:
                for odd in (1, 0):
                    steps(2 * pair + 2 - odd, body_steps(True, True), (odd + 1) % 2 if False else odd)
            steps(NG - 1, body_steps(False, True))

        block = stack.enter_context(nc.Block())

        FBp = FB[:, :, :].rearrange("p k (a h n) -> p k a h n", a=2, h=2)

        def fb_of(bank):
            return bank[:, 0:KD * 64].rearrange("p (k a n) -> p k a n", k=KD, a=2)

        def piece_place(j):
            if j < NFF:
                return fcT[:, :, j * P:(j + 1) * P]
            t, q = (j - NFF) // 4, (j - NFF) % 4
            return projT[:, 4 * q:4 * q + 4, t * P:(t + 1) * P]

        def piece_bank(j):
            return banks[f"O{j % 4}"][:, 0:256].bitcast(BF16).rearrange("p (k n) -> p k n", k=4)

        @block.sync
        def _(sp):
            sp.dma_start(Wq_s[:, :, :], Wq.rearrange("(c p) e -> p c e", p=P)).then_inc(wq_in, 16)

            def ring_load(k):
                src = (w_fc.rearrange("(k p) d -> k p d", p=P)[k] if k < NFF
                       else w_proj.rearrange("(t p) (c d) -> t p c d", p=P, d=D)[(k - NFF) // 4][:, k % 4, :])
                sp.dma_start(wring[:, k // 4 % 2, k % 4, :], src).then_inc(ring_in[k % 8], 16)

            def load_next(b):
                sp.wait_ge(n1_made, 4 * (b + 2))
                sp.wait_ge(res_made, 4 * (b + 2))
                sp.dma_start(xb[:, :, :].rearrange("p (c t) d -> p c (t d)", c=2), x_in[b + 2]).then_inc(x_in_s, 16)
                sp.wait_ge(unit_full, n_full(b, ("n2T", 3)))
                sp.dma_start(ctxb[:, :, :].rearrange("p (c t) d -> p c (t d)", c=2), ctx_in[b + 2]).then_inc(ctx_in_s, 16)

            def store(g, tiles_of):
                for c in range(2):
                    sp.wait_ge(y_added, 4 * g + 2 * c + 2)
                    sp.dma_start(out_v[g, c], x2[tiles_of][:, 2 * c:2 * c + 2, :].rearrange("p t d -> p (t d)")
                                 ).then_inc(stored, 16)

            for k in range(2):
                ring_load(k)
            sp.dma_start(Wk_s[:, :, :], Wk.rearrange("(c p) e -> p c e", p=P)).then_inc(wk_in, 16)
            for k in range(2, 4):
                ring_load(k)
            sp.dma_start(xb[:, :, :].rearrange("p (c t) d -> p c (t d)", c=2), x_in[0]).then_inc(x_in_s, 16)
            for k in range(4, 8):
                ring_load(k)
            sp.dma_start(ctxb[:, :, :].rearrange("p (c t) d -> p c (t d)", c=2), ctx_in[0]).then_inc(ctx_in_s, 16)
            sp.dma_start(Wv_s[:, :, :], Wv.rearrange("(c p) e -> p c e", p=P)).then_inc(wv_in, 16)
            sp.dma_start(Wo_s[:, :, :], Wo.rearrange("(c p) e -> p c e", p=P)).then_inc(wo_in, 16)
            sp.dma_start(borow, bo.partition_broadcast(P)).then_inc(vbias_in, 16)
            sp.dma_start(gatec[:, :], gate.partition_broadcast(P)).then_inc(lowrank_in, 16)
            sp.dma_start(v_s, v).then_inc(lowrank_in, 16)
            for i in range(4):
                sp.dma_start(fbT4[:, i, :], fast_b.rearrange("r s -> s r"), allow_slow_non_contiguous=True
                             ).then_inc(lowrank_in, 16)
            sp.dma_start(u_s[:, :, :], u.rearrange("(c p) r -> p c r", p=P)).then_inc(lowrank_in, 16)
            for k in range(8, PIECES):
                sp.wait_ge(tern_made, k - 7)
                ring_load(k)
            load_next(-1)
            load_next(0)
            with sp.Fori(0, 2) as pair:
                for odd in (1, 0):
                    store(2 * pair + 1 - odd, 1 - odd)
                    load_next(2 * pair + 2 - odd)
            store(4, 0)
            load_next(5)
            store(5, 1)
            store(6, 0)
            store(7, 1)
            sp.wait_ge(stored, 32 * NG)

        @block.gpsimd
        def _(pool):
            nc.gpsimd.memset(ident[:, :], 0.0).then_inc(pool_own, 1)
            pool.wait_ge(pool_own, 1)
            nc.gpsimd.affine_select(out=ident[:, :], in_=ident[:, :], compare_op=ALU.not_equal, fill=1.0, base=0,
                                    pattern=[[-1, P]], channel_multiplier=1).then_inc(pool_own, 1)
            nc.gpsimd.memset(ones[:, :], 1.0).then_inc(const_ready, 1)
            nc.gpsimd.memset(mhalf[:, :], -0.5).then_inc(pool_own, 1)
            pool.wait_ge(pool_own, 3)
            nc.gpsimd.tensor_copy(identb[:, :], ident[:, :]).then_inc(const_ready, 1)

            def steps(b, todo, odd=None):
                g = b + 1
                par = 0 if isinstance(b, int) and b < 0 else (odd + 1) % 2 if odd is not None else (b + 1) % 2
                for st in todo:
                    roots = {"xs23": (0, xrs[:, :]), "cs23": (1, crs[:, :])}
                    roots.update({("a", t): (2 + t, nrs[:, t:t + 1]) for t in range(TILES)})
                    if st in roots:
                        n, var = roots[st]
                        pool.wait_ge(var_made, NROOT * g + n + 1)
                        nc.gpsimd.tensor_tensor(var, var, mhalf[:, 0:var.shape[1]], ALU.pow).then_inc(rstd_made, 1)
                    elif st == "residual":
                        pool.wait_ge(x_in_s, 16 * (g + 1))
                        if isinstance(b, int) and b < 0:
                            pool.wait_ge(job_dve, job_count(JOBS.index(("co", 0)), "dve"))
                        elif isinstance(b, int) and b == 0:
                            pool.wait_ge(ut_full, 4)
                        else:
                            pool.wait_ge(stored, 32 * b)
                        for t in range(TILES):
                            nc.gpsimd.tensor_tensor(x2[par][:, t, :], xb[:, t, :], crow[:, :],
                                                    ALU.add).then_inc(res_made, 1)
                    elif st == "out23":
                        for t in range(TILES):
                            pool.wait_ge(y_made, 4 * (b - 1) + t + 1)
                            nc.gpsimd.tensor_tensor(x2[par][:, t, :], x2[par][:, t, :], ybuf[t],
                                                    ALU.add).then_inc(y_added, 1)
            run_bodies(pool, steps)
            for t in range(TILES):
                pool.wait_ge(y_made, 4 * (NG - 1) + t + 1)
                nc.gpsimd.tensor_tensor(x2[1][:, t, :], x2[1][:, t, :], ybuf[t], ALU.add).then_inc(y_added, 1)

        @block.scalar
        def _(act):
            def columns(dst, src, to):
                act.dma_start(dst[:, :], src.rearrange("(c p) -> p c", p=P), allow_slow_non_contiguous=True
                              ).then_inc(to, 16)

            columns(g2c, ln2_g, gains_in)
            columns(g1c, ln1_g, gains_in)
            columns(b1c, ln1_b, qbias_in)
            columns(bqc, bq, qbias_in)
            columns(b2c, ln2_b, vbias_in)
            columns(bvc, bv, vbias_in)

            def job(n):
                kind, c = JOBS[n]
                if "act" not in job_engines(n):
                    return
                bank = banks[f"H{n % 2}"]
                act.wait_ge(job_full, n + 1)
                if kind == "wqT":
                    nc.scalar.activation(WqT[:, :, c * P:(c + 1) * P], bank[:, :].rearrange("p (k n) -> p k n", k=KE),
                                         ACT.Copy).then_inc(job_act, 1)
                elif kind == "wkT":
                    nc.scalar.activation(WkT[:, :, c * P:(c + 1) * P], bank[:, :].rearrange("p (k n) -> p k n", k=KE),
                                         ACT.Copy).then_inc(job_act, 1)
                elif kind == "wvT":
                    nc.scalar.activation(WvT[:, :, c * P:(c + 1) * P], bank[:, :].rearrange("p (k n) -> p k n", k=KE),
                                         ACT.Copy).then_inc(job_act, 1)
                elif kind == "M":
                    act.wait_ge(gains_in, 32)
                    nc.scalar.activation(M[:, HI, c, :], bank[:, 0:DC], ACT.Copy, scale=g1c[:, c:c + 1]
                                         ).then_inc(job_act, 1)
                elif kind == "wvo":
                    nc.scalar.activation(Wvo[:, HI, c, :], bank[:, :], ACT.Copy, scale=g2c[:, c:c + 1]
                                         ).then_inc(job_act, 1)
                elif kind == "fb":
                    nc.scalar.activation(FBp[:, :, :, HI, :], fb_of(bank), ACT.Copy).then_inc(job_act, 1)

            def unit(b, un):
                kind, t = un
                if kind == "a":
                    return
                bank = banks[bank_of(b, un)]
                wide = bank[:, :].rearrange("p (k n) -> p k n", k=4)
                cols = slice(t * P, (t + 1) * P)
                if kind == "s":
                    if un == ("s", 0) and not (isinstance(b, int) and b <= 0):
                        act.wait_ge(y_added, 4 * b)
                    act.wait_ge(unit_dve, n_dve(b, un))
                    nc.scalar.activation(pbuf[:, t, :], bank[:, 0:S], ACT.Exp, bias=nmax[:, t:t + 1], scale=SM,
                                         accum_out=rowsum[:, t:t + 1]).then_inc(unit_act, 1)
                    return
                act.wait_ge(unit_full, n_full(b, un))
                if kind == "x":
                    if isinstance(b, int) and b == 0 and t == 0:
                        act.wait_ge(tern_made, PIECES)
                    nc.scalar.activation(xnT[:, HI, :, cols], wide, ACT.Copy).then_inc(unit_act, 1)
                elif kind == "L":
                    nc.scalar.activation(tstack[:, :], bank[:, :], ACT.Copy).then_inc(unit_act, 1)
                elif kind == "n1T":
                    nc.scalar.activation(n1T[:, HI, :, cols], wide, ACT.Copy).then_inc(unit_act, 1)
                elif kind == "n2T":
                    nc.scalar.activation(n2T[:, HI, :, cols], wide[:, 0:KC, :], ACT.Copy).then_inc(unit_act, 1)
                elif kind == "t":
                    nc.scalar.activation(tT[:, HI, t, :], bank[:, :], ACT.Identity, bias=tbias[:, t:t + 1]
                                         ).then_inc(unit_act, 1)
                elif kind == "v":
                    nc.scalar.activation(vo[:, HI, t, :], bank[:, :], ACT.Copy).then_inc(unit_act, 1)
                elif kind == "pT":
                    nc.scalar.activation(pT[:, HI, t, :, :], bank[:, :].rearrange("p (j q) -> p j q", j=2),
                                         ACT.Copy).then_inc(unit_act, 1)

            def steps(b, todo, odd=None):
                for st in todo:
                    if isinstance(st, str):
                        continue
                    kind, j = st
                    if kind in ("x", "L", "n1T", "n2T", "t", "s", "v", "pT", "a"):
                        unit(b, st)
                    elif kind == "up":
                        act.wait_ge(up_full, NFF * b + j + 1)
                        if not (isinstance(b, int) and b == 0 and j < 2):
                            act.wait_ge(sqlo_made, NFF * b + j - 1)
                        nc.scalar.activation(rbuf[:, j % 2, :], banks[f"H{j % 2}"][:, :], ACT.Relu,
                                             scale=scf[:, j:j + 1]).then_inc(relu_made, 1)
                    elif kind == "hi":
                        act.wait_ge(square_made, NFF * b + j + 1)
                        if not (isinstance(b, int) and b == 0 and j < 2):
                            act.wait_ge(down_full, NFF * b + j - 1)
                        nc.scalar.activation(qbuf[:, j % 2, HI, :], rbuf[:, j % 2, :], ACT.Copy
                                             ).then_inc(sqhi_made, 1)
                    elif kind == "job":
                        job(j)
                    elif kind == "abs":
                        act.wait_ge(ring_in[j % 8], 16 * (j // 8 + 1))
                        if j >= 2:
                            act.wait_ge(abs_done, j - 1)
                        nc.scalar.activation(absj[:, j % 2, :], wring[:, j // 4 % 2, j % 4, :], ACT.Abs,
                                             accum_out=asum[:, j // 4, j % 4:j % 4 + 1]).then_inc(abs_done, 1)
                    elif kind == "sign":
                        gr, i = j // 4, j % 4
                        at = i if gr < 4 else 0
                        act.wait_ge(scales_made, gr + 1)
                        if j >= 2:
                            act.wait_ge(tern_made, j - 1)
                        nc.scalar.activation(signs[:, j % 2, :], wring[:, gr % 2, i, :], ACT.Sign,
                                             bias=half[:, gr % 2, at:at + 1]).then_inc(signs_made, 1)
                    elif kind == "store" and j % 2 == 0:
                        act.wait_ge(tern_turned, j + 1)
                        nc.scalar.activation(piece_place(j), piece_bank(j), ACT.Copy).then_inc(even_stored, 1)
                    elif kind == "ut":
                        act.wait_ge(ut_full, j + 1)
                        nc.scalar.activation(uT[:, j * 512:(j + 1) * 512], banks[f"O{(j + 23) % 4}"][:, :], ACT.Copy
                                             ).then_inc(ut_stored, 1)
            run_bodies(act, steps)

        @block.vector
        def _(dve):
            OWN_PRO, OWN_BODY = [None], [None]
            chain = {"base": 0, "n": 0}

            def link(ins):
                chain["n"] += 1
                ins.then_inc(own, 1)
                dve.wait_ge(own, chain["base"] + chain["n"])

            def link_to_aggr(ins):
                link(ins)
                nc.vector.memset(spare[:, :], 0.0)

            def job(n):
                kind, c = JOBS[n]
                if "dve" not in job_engines(n):
                    return
                bank = banks[f"H{n % 2}"]
                dve.wait_ge(job_full, n + 1)
                wide = bank[:, :].rearrange("p (k n) -> p k n", k=KE)
                if kind == "wqT":
                    nc.vector.tensor_copy(WqT[:, :, c * P:(c + 1) * P], wide).then_inc(job_dve, 1)
                elif kind == "wkT":
                    nc.vector.tensor_copy(WkT[:, :, c * P:(c + 1) * P], wide).then_inc(job_dve, 1)
                elif kind == "wvT":
                    nc.vector.tensor_copy(WvT[:, :, c * P:(c + 1) * P], wide).then_inc(job_dve, 1)
                elif kind == "bq":
                    dve.wait_ge(qbias_in, 16 * 2)
                    nc.vector.tensor_tensor(bqp[:, :], bank[:, 0:KE], bqc[:, :], ALU.add).then_inc(job_dve, 1)
                elif kind == "bv":
                    dve.wait_ge(const_ready, 2)
                    dve.wait_ge(vbias_in, 16 * 3)
                    link(nc.vector.tensor_tensor(bvp[:, :], bank[:, 0:KE], bvc[:, :], ALU.add))
                    for k in range(KE):
                        last = nc.vector.tensor_scalar(bvrep[:, k, :], ones[:, :], bvp[:, k:k + 1], None, ALU.mult)
                    last.then_inc(job_dve, 1)
                elif kind == "M":
                    dve.wait_ge(job_act, job_count(n, "act"))
                    nc.vector.scalar_tensor_tensor(out=M[:, LO, c, :], in0=bank[:, 0:DC], scalar=g1c[:, c:c + 1],
                                                   in1=M[:, HI, c, :], op0=ALU.mult, op1=ALU.subtract
                                                   ).then_inc(job_dve, 1)
                elif kind == "tb":
                    nc.vector.tensor_copy(tbias[:, :], bank[:, 0:KC]).then_inc(job_dve, 1)
                elif kind == "wvo":
                    dve.wait_ge(job_act, job_count(n, "act"))
                    nc.vector.scalar_tensor_tensor(out=Wvo[:, LO, c, :], in0=bank[:, :], scalar=g2c[:, c:c + 1],
                                                   in1=Wvo[:, HI, c, :], op0=ALU.mult, op1=ALU.subtract
                                                   ).then_inc(job_dve, 1)
                elif kind == "co":
                    nc.vector.tensor_tensor(crow[:, :], bank[:, :], borow, ALU.add).then_inc(job_dve, 1)
                elif kind == "fb":
                    dve.wait_ge(job_act, job_count(n, "act"))
                    nc.vector.tensor_tensor(FBp[:, :, :, LO, :], fb_of(bank), FBp[:, :, :, HI, :], ALU.subtract).then_inc(job_dve, 1)
            def unit(b, un):
                kind, t = un
                bank = banks[bank_of(b, un)]
                wide = bank[:, :].rearrange("p (k n) -> p k n", k=4)
                cols = slice(t * P, (t + 1) * P)
                if kind == "s":
                    dve.wait_ge(unit_full, n_full(b, un))
                    link(nc.vector.tensor_reduce(rowmax[:, t:t + 1], bank[:, 0:S], AX_X, ALU.max))
                    nc.vector.tensor_scalar(nmax[:, t:t + 1], rowmax[:, t:t + 1], -SM, None, ALU.mult
                                            ).then_inc(unit_dve, 1)
                    return
                if kind == "a":
                    dve.wait_ge(unit_full, n_full(b, un))
                    dve.wait_ge(res_made, 4 * (b + 1) + t + 1)
                    here = x2[cur["par"]]
                    nc.vector.scalar_tensor_tensor(out=here[:, t, :], in0=bank[:, :], scalar=rinv[:, t:t + 1],
                                                   in1=here[:, t, :], op0=ALU.mult, op1=ALU.add
                                                   ).then_inc(unit_dve, 1)
                    dve.wait_ge(unit_dve, n_dve(b, un))
                    link_to_aggr(nc.vector.bn_stats(nst[:, t, :], here[:, t, :]))
                    link(nc.vector.bn_aggr(nmv[:, t, :], nst[:, t, :]))
                    nc.vector.tensor_scalar(nrs[:, t:t + 1], nmv[:, t, 1:2], EPS, None, ALU.add).then_inc(var_made, 1)
                    return
                dve.wait_ge(unit_act, n_act(b, un))
                if kind == "x":
                    nc.vector.tensor_tensor(xnT[:, LO, :, cols], wide, xnT[:, HI, :, cols], ALU.subtract
                                            ).then_inc(unit_dve, 1)
                elif kind == "L":
                    nc.vector.tensor_tensor(tstack[64:128, :], bank[64:128, :], tstack[64:128, :], ALU.subtract
                                            ).then_inc(unit_dve, 1)
                elif kind == "n1T":
                    nc.vector.tensor_tensor(n1T[:, LO, :, cols], wide, n1T[:, HI, :, cols], ALU.subtract
                                            ).then_inc(unit_dve, 1)
                elif kind == "n2T":
                    nc.vector.tensor_tensor(n2T[:, LO, :, cols], wide[:, 0:KC, :], n2T[:, HI, :, cols], ALU.subtract
                                            ).then_inc(unit_dve, 1)
                elif kind == "t":
                    nc.vector.scalar_tensor_tensor(out=tT[:, LO, t, :], in0=bank[:, :], scalar=tbias[:, t:t + 1],
                                                   in1=tT[:, HI, t, :], op0=ALU.add, op1=ALU.subtract
                                                   ).then_inc(unit_dve, 1)
                elif kind == "v":
                    nc.vector.tensor_tensor(vo[:, LO, t, :], bank[:, :], vo[:, HI, t, :], ALU.subtract
                                            ).then_inc(unit_dve, 1)
                elif kind == "pT":
                    nc.vector.tensor_tensor(pT[:, LO, t, :, :], bank[:, :].rearrange("p (j q) -> p j q", j=2),
                                            pT[:, HI, t, :, :], ALU.subtract).then_inc(unit_dve, 1)
                    link(nc.vector.reciprocal(rinv[:, 2 * t:2 * t + 2], rowsum[:, 2 * t:2 * t + 2]))

            cur = {"par": 0}

            def evacuate(g, t):
                if t == 0:
                    dve.wait_ge(down_full, NFF * (g + 1))
                if isinstance(g, int) and g == NG - 1:
                    dve.wait_ge(y_added, 4 * g)
                elif t >= 2:
                    dve.wait_ge(unit_full, n_full(g + 1, ("x", t)))
                nc.vector.tensor_tensor(ybuf[t], banks[f"O{t}"][:, :], sprow[:, :], ALU.mult).then_inc(y_made, 1)

            def steps(b, todo, odd=None):
                first = isinstance(b, int) and b < 0
                g = b + 1
                cur["par"] = 0 if first else (odd + 1) % 2 if odd is not None else (b + 1) % 2
                prev = 1 - cur["par"]
                if first:
                    chain["base"] = 0
                    chain["pro"] = None
                else:
                    if chain["pro"] is None:
                        chain["pro"] = chain["n"]
                    chain["base"] = chain["pro"] + PER_BODY * b
                    chain["n"] = 0
                for st in todo:
                    kind, j = st if isinstance(st, tuple) else (st, None)
                    if kind in ("x", "L", "n1T", "n2T", "t", "s", "v", "pT", "a"):
                        unit(b, st)
                    elif kind == "job":
                        job(j)
                    elif kind == "gainK":
                        dve.wait_ge(gains_in, 32)
                        dve.wait_ge(wk_in, 16)
                        for k in range(KC):
                            last = nc.vector.tensor_scalar(Wk_s[:, k, :], Wk_s[:, k, :], g2c[:, k:k + 1], None,
                                                           ALU.mult)
                        last.then_inc(gained, 1)
                    elif kind in ("xs01", "xs23"):
                        if kind == "xs01":
                            dve.wait_ge(x_in_s, 16 * (g + 1))
                        for t in (0, 1) if kind == "xs01" else (2, 3):
                            last = nc.vector.bn_stats(xst[:, t, :], xb[:, t, :])
                        if kind == "xs23":
                            link_to_aggr(last)
                            for t in range(TILES):
                                last = nc.vector.bn_aggr(xmv[:, t, :], xst[:, t, :])
                            link(last)
                            nc.vector.tensor_scalar(xrs[:, :], xmv[:, :, 1], 1.0 + EPS, EPS * EPS, ALU.mult,
                                                    ALU.add).then_inc(var_made, 1)
                    elif kind in ("cs01", "cs23"):
                        if kind == "cs01":
                            dve.wait_ge(ctx_in_s, 16 * (g + 1))
                        for t in (0, 1) if kind == "cs01" else (2, 3):
                            last = nc.vector.bn_stats(cst[:, t, :], ctxb[:, t, :])
                        if kind == "cs23":
                            link_to_aggr(last)
                            for t in range(TILES):
                                last = nc.vector.bn_aggr(cmv[:, t, :], cst[:, t, :])
                            link(last)
                            nc.vector.tensor_scalar(crs[:, :], cmv[:, :, 1], EPS, None, ALU.add
                                                    ).then_inc(var_made, 1)
                    elif kind[:2] == "nx":
                        t = int(kind[2])
                        if t >= 2:
                            dve.wait_ge(unit_full, n_full(b, ("n1T", t - 2)))
                        elif isinstance(b, int) and b == 0:
                            dve.wait_ge(unit_full, n_full(b, ("x", t + 2)))
                        elif not first:
                            dve.wait_ge(y_added, 4 * b)
                        if t == 0:
                            dve.wait_ge(rstd_made, NROOT * g + 1)
                        nc.vector.tensor_scalar(nrm[:, t % 2, :], xb[:, t, :], xmv[:, t, 0:1], xrs[:, t:t + 1],
                                                ALU.subtract, ALU.mult).then_inc(n1_made, 1)
                    elif kind[:2] == "nc":
                        t = int(kind[2])
                        if t == 0:
                            dve.wait_ge(rstd_made, NROOT * g + 2)
                        nc.vector.tensor_scalar(ctxb[:, t, :], ctxb[:, t, :], cmv[:, t, 0:1], crs[:, t:t + 1],
                                                ALU.subtract, ALU.mult).then_inc(n2_made, 1)
                    elif kind[:2] == "nX":
                        t = int(kind[2])
                        here = cur["par"] if t < 2 else prev
                        dve.wait_ge(rstd_made, NROOT * (g if t < 2 else b) + 3 + t)
                        if t >= 2:
                            dve.wait_ge(unit_full, n_full(b, ("x", t - 2)))
                        nc.vector.tensor_scalar(nrm[:, t % 2, :], x2[here][:, t, :], nmv[:, t, 0:1], nrs[:, t:t + 1],
                                                ALU.subtract, ALU.mult).then_inc(xn_made, 1)
                    elif kind in ("out01", "out23"):
                        for t in (0, 1) if kind == "out01" else (2, 3):
                            evacuate(b - 1, t)
                    elif kind == "sq":
                        dve.wait_ge(relu_made, NFF * b + j + 1)
                        nc.vector.tensor_tensor(rbuf[:, j % 2, :], rbuf[:, j % 2, :], rbuf[:, j % 2, :], ALU.mult
                                                ).then_inc(square_made, 1)
                    elif kind == "lo":
                        dve.wait_ge(sqhi_made, NFF * b + j + 1)
                        nc.vector.tensor_tensor(qbuf[:, j % 2, LO, :], rbuf[:, j % 2, :], qbuf[:, j % 2, HI, :],
                                                ALU.subtract).then_inc(sqlo_made, 1)
                    elif kind == "scale":
                        dve.wait_ge(abs_done, 4 * j + 4)
                        if j < 4:
                            sc, n = scf[:, 4 * j:4 * j + 4], 4
                            link(nc.vector.tensor_scalar(sc, asum[:, j, :], 1.0 / D, EPS, ALU.mult, ALU.max))
                        else:
                            sc, n = spc[:, j - 4:j - 3], 1
                            link(nc.vector.tensor_reduce(psum4[:, j - 4:j - 3], asum[:, j, :], AX_X, ALU.add))
                            link(nc.vector.tensor_scalar(sc, psum4[:, j - 4:j - 3], 1.0 / HID, EPS, ALU.mult, ALU.max))
                        nc.vector.tensor_scalar(half[:, j % 2, 0:n], sc, 0.5, None, ALU.mult
                                                ).then_inc(scales_made, 1)
                        dve.wait_ge(scales_made, j + 1)
                    elif kind == "tern":
                        gr, i = j // 4, j % 4
                        at = i if gr < 4 else 0
                        w = wring[:, gr % 2, i, :]
                        if j >= 4:
                            dve.wait_ge(tern_turned, j - 3)
                        dve.wait_ge(signs_made, j + 1)
                        nc.vector.scalar_tensor_tensor(out=tern[:, i, :], in0=w, scalar=half[:, gr % 2, at:at + 1],
                                                       in1=signs[:, j % 2, :], op0=ALU.is_gt, op1=ALU.min
                                                       ).then_inc(tern_made, 1)
                    elif kind == "store" and j % 2 == 1:
                        dve.wait_ge(tern_turned, j + 1)
                        nc.vector.tensor_copy(piece_place(j), piece_bank(j)).then_inc(odd_stored, 1)
                    elif kind == "uprep":
                        dve.wait_ge(lowrank_in, 16 * 7)
                        link(nc.vector.reciprocal(urs[:, :], scf[:, :]))
                        link(nc.vector.tensor_scalar(urs[:, :], urs[:, :], gatec[:, 0:1], None, ALU.mult))
                        link(nc.vector.tensor_tensor(u_s[:, :, :], u_s[:, :, :],
                                                     urs[:, :].unsqueeze(2).broadcast_to([P, NFF, RK]), ALU.mult))
                        link(nc.vector.tensor_copy(uhi[:, :, :], u_s[:, :, :]))
                        for i in range(4):
                            nc.vector.tensor_copy(unat[:, :, 2 * i, :], uhi[:, :, :])
                            last = nc.vector.tensor_tensor(unat[:, :, 2 * i + 1, :], u_s[:, :, :], uhi[:, :, :],
                                                           ALU.subtract)
                        last.then_inc(unat_made, 1)
                    elif kind == "diag":
                        for t in range(KD):
                            last = nc.vector.tensor_scalar(bvrep[:, t, :], ident[:, :], spc[:, t:t + 1], None, ALU.mult)
                        last.then_inc(diag_made, 1)
                    elif kind == "sprow_out":
                        dve.wait_ge(sprow_full, 1)
                        nc.vector.tensor_copy(sprow[:, :], banks["O0"][:, :]).then_inc(sprow_made, 1)
                        dve.wait_ge(sprow_made, 1)
                if not first and not (isinstance(b, int) and b == NG - 1):
                    assert chain["n"] == PER_BODY, chain["n"]

            PER_BODY = 2 + 2 + 4 + 8 + 2
            run_bodies(dve, steps)
            for t in range(TILES):
                evacuate(NG - 1, t)

        @block.tensor
        def _(pe):
            pe.wait_ge(const_ready, 2)

            def job(n):
                kind, c = JOBS[n]
                bank = banks[f"H{n % 2}"]
                if n >= 2:
                    job_read(pe, n - 2)
                if kind in ("wqT", "wkT", "wvT"):
                    if kind == "wqT":
                        pe.wait_ge(wq_in, 16)
                    elif kind == "wkT":
                        pe.wait_ge(gained, 1)
                    else:
                        pe.wait_ge(wv_in, 16)
                    w = {"wqT": Wq_s, "wkT": Wk_s, "wvT": Wv_s}[kind]
                    for k in range(KE):
                        mm = pe.transpose(bank[:, k * P:(k + 1) * P], w[:, c, k * P:(k + 1) * P], ident[:, :])
                elif kind == "bq":
                    pe.wait_ge(qbias_in, 16 * 2)
                    for e in range(KE):
                        for k in range(KD):
                            mm = pe.matmul(bank[:, e:e + 1], Wq_s[:, k, e * P:(e + 1) * P], b1c[:, k:k + 1],
                                           start=(k == 0), stop=(k == KD - 1))
                elif kind == "bv":
                    pe.wait_ge(vbias_in, 16 * 3)
                    for e in range(KE):
                        for k in range(KC):
                            mm = pe.matmul(bank[:, e:e + 1], Wv_s[:, k, e * P:(e + 1) * P], b2c[:, k:k + 1],
                                           start=(k == 0), stop=(k == KC - 1))
                elif kind == "M":
                    if c == 0:
                        for last in (KD + KC - 2, KD + KC - 1):
                            job_read(pe, last)
                    for k in range(KE):
                        mm = pe.matmul(bank[:, 0:DC], WqT[:, k, c * P:(c + 1) * P], WkT[:, k, :],
                                       start=(k == 0), stop=(k == KE - 1))
                elif kind == "tb":
                    job_read(pe, JOBS.index(("bq", 0)))
                    for m in range(KC):
                        for k in range(KE):
                            mm = pe.matmul(bank[:, m:m + 1], WkT[:, k, m * P:(m + 1) * P], bqp[:, k:k + 1],
                                           start=(k == 0), stop=(k == KE - 1))
                elif kind == "wvo":
                    if c == 0:
                        pe.wait_ge(wo_in, 16)
                        for last in (JOBS.index(("wvT", KC - 2)), JOBS.index(("wvT", KC - 1))):
                            job_read(pe, last)
                    for k in range(KE):
                        mm = pe.matmul(bank[:, :], WvT[:, k, c * P:(c + 1) * P], Wo_s[:, k, :],
                                       start=(k == 0), stop=(k == KE - 1))
                elif kind == "co":
                    job_read(pe, JOBS.index(("bv", 0)))
                    for k in range(KE):
                        mm = pe.matmul(bank[:, :], bvrep[:, k, :], Wo_s[:, k, :], start=(k == 0), stop=(k == KE - 1))
                elif kind == "fb":
                    pe.wait_ge(lowrank_in, 16 * 7)
                    for k in range(KD):
                        mm = pe.matmul(bank[:, k * 64:(k + 1) * 64], v_s[:, k * P:(k + 1) * P],
                                       fbT4[:, :, :].rearrange("s i r -> s (i r)"), start=True, stop=True)
                mm.then_inc(job_full, 1)

            def products(bank, pairs):
                for i, (w, m) in enumerate(pairs):
                    mm = pe.matmul(bank, w, m, start=(i == 0), stop=(i == len(pairs) - 1))
                return mm

            THREE = [(HI, HI), (HI, LO), (LO, HI)]

            def unit(b, un):
                kind, t = un
                name = bank_of(b, un)
                bank = banks[name]
                before = bank_before(b, un)
                cols = slice(t * P, (t + 1) * P)
                if isinstance(b, int) and b < 0 and name[0] == "H" and before is None:
                    job_read(pe, len(JOBS) - 2 if name == "H0" else len(JOBS) - 1)
                elif un in (("x", 2), ("x", 3)) and not (isinstance(b, int) and b == 0):
                    pe.wait_ge(relu_made, NFF * (b - 1) + NFF - 1 + (t == 3))
                elif before:
                    if before[1][0] == "s":
                        pe.wait_ge(unit_act, n_act(*before))
                    else:
                        pe.wait_ge(unit_dve, n_dve(*before))
                if kind in ("x", "n1T", "n2T"):
                    src, made = {"x": (nrm[:, t % 2, :], xn_made), "n1T": (nrm[:, t % 2, :], n1_made),
                                 "n2T": (ctxb[:, t, :], n2_made)}[kind]
                    pe.wait_ge(made, 4 * (b if kind == "x" else b + 1) + t + 1)
                    for k in range(KC if kind == "n2T" else KD):
                        mm = pe.transpose(bank[:, k * P:(k + 1) * P], src[:, k * P:(k + 1) * P], ident[:, :])
                elif kind == "L":
                    if isinstance(b, int) and b == 0:
                        job_read(pe, JOBS.index(("fb", 0)))
                    pe.wait_ge(unit_dve, n_dve(b, ("x", 3)))
                    mm = products(bank[:, :], [(FB[:, k, :], xnT[:, h, k, :]) for k in range(KD) for h in (HI, LO)])
                elif kind == "t":
                    if isinstance(b, int) and b < 0 and t == 0:
                        job_read(pe, JOBS.index(("M", KD - 1)))
                    pe.wait_ge(unit_dve, n_dve(b, ("n1T", 3)))
                    mm = products(bank[:, :], [(M[:, w, k, cols], n1T[:, m, k, :]) for k in range(KD) for w, m in THREE])
                elif kind == "s":
                    c = t // 2
                    if t == 0:
                        pe.wait_ge(unit_dve, n_dve(b, ("t", 2)))
                    mm = products(bank[:, 0:S], [(tT[:, w, k, cols], n2T[:, m, k, c * S:(c + 1) * S])
                                                 for k in range(KC) for w, m in THREE])
                elif kind == "v":
                    if isinstance(b, int) and b < 0 and t == 0:
                        job_read(pe, JOBS.index(("wvo", KC - 1)))
                    mm = products(bank[:, :], [(n2T[:, w, k, cols], Wvo[:, m, k, :]) for k in range(KC)
                                               for w, m in THREE])
                elif kind == "pT":
                    pe.wait_ge(unit_act, n_act(b, ("s", 2 * t + 1)))
                    for j in range(2):
                        for q in range(2):
                            mm = pe.transpose(bank[:, j * S + q * P:j * S + (q + 1) * P],
                                              pbuf[:, 2 * t + q, j * P:(j + 1) * P], ident[:, :])
                elif kind == "a":
                    c, q = t // 2, t % 2
                    pe.wait_ge(unit_dve, max(n_dve(-1, ("v", 2 * c + 1)), n_dve(-1, ("pT", c)))
                               if isinstance(b, int) and b < 0 else n_dve(b, ("pT", c)))
                    mm = products(bank[:, :], [(pT[:, w, c, j, q * P:(q + 1) * P], vo[:, m, 2 * c + j, :])
                                               for j in range(2) for w, m in THREE])
                mm.then_inc(unit_full, 1)

            def turn_free(j):
                if j >= 4:
                    pe.wait_ge(odd_stored if j % 2 else even_stored, (j - 4) // 2 + 1)

            def down(b, j):
                pe.wait_ge(sqlo_made, NFF * b + j + 1)
                if j == 0:
                    if isinstance(b, int) and b == 0:
                        pe.wait_ge(even_stored, PIECES // 2)
                        pe.wait_ge(odd_stored, PIECES // 2)
                        pe.wait_ge(sprow_made, 1)
                    else:
                        pe.wait_ge(y_made, 4 * b)
                for t in range(TILES):
                    for h in (HI, LO):
                        mm = pe.matmul(banks[f"O{t}"][:, :], qbuf[:, j % 2, h, t * P:(t + 1) * P], projT[:, j, :],
                                       start=(j == 0 and h == HI), stop=(j == NFF - 1 and h == LO))
                mm.then_inc(down_full, 1)

            def steps(b, todo, odd=None):
                for st in todo:
                    kind, j = st if isinstance(st, tuple) else (st, None)
                    if kind in ("x", "L", "n1T", "n2T", "t", "s", "v", "pT", "a"):
                        unit(b, st)
                    elif kind == "job":
                        job(j)
                    elif kind == "up":
                        if j == 0:
                            pe.wait_ge(unit_dve, n_dve(b, ("x", 3)))
                        elif j >= 2:
                            pe.wait_ge(relu_made, NFF * b + j - 1)
                        for k in range(KD):
                            for h in (HI, LO):
                                pe.matmul(banks[f"H{j % 2}"][:, :], fcT[:, k, j * P:(j + 1) * P], xnT[:, h, k, :],
                                          start=(k == 0 and h == HI), stop=False)
                        if j == 0:
                            pe.wait_ge(unit_dve, n_dve(b, ("L", 0)))
                            if isinstance(b, int) and b == 0:
                                pe.wait_ge(ut_stored, 4)
                        pe.matmul(banks[f"H{j % 2}"][:, :], uT[:, j * P:(j + 1) * P], tstack[:, :],
                                  start=False, stop=True).then_inc(up_full, 1)
                    elif kind == "down":
                        down(b, j)
                    elif kind == "down-":
                        down(b - 1, j)
                    elif kind == "turn":
                        pe.wait_ge(tern_made, j + 1)
                        turn_free(j)
                        if j >= 23:
                            pe.wait_ge(ut_stored, min(j - 22, 4))
                        ps = banks[f"O{j % 4}"][:, 0:256].bitcast(BF16)
                        for k in range(4):
                            mm = pe.transpose(ps[:, k * P:(k + 1) * P], tern[:, j % 4, k * P:(k + 1) * P], identb[:, :])
                        mm.then_inc(tern_turned, 1)
                    elif kind == "ut":
                        if j == 0:
                            pe.wait_ge(unat_made, 1)
                        turn_free(j + 23)
                        for i in range(4):
                            mm = pe.transpose(banks[f"O{(j + 23) % 4}"][:, i * P:(i + 1) * P],
                                              unat[:, 4 * j + i, :, :].rearrange("p i r -> p (i r)"), ident[:, :])
                        mm.then_inc(ut_full, 1)
                    elif kind == "sprow":
                        pe.wait_ge(diag_made, 1)
                        pe.wait_ge(even_stored, PIECES // 2 - 1)
                        for t in range(KD):
                            mm = pe.matmul(banks["O0"][:, t * P:(t + 1) * P], ones[:, :], bvrep[:, t, :],
                                           start=True, stop=True)
                        mm.then_inc(sprow_full, 1)

            run_bodies(pe, steps, "pe")
            for j in (NFF - 2, NFF - 1):
                down(NG - 1, j)


_INS = ['x', 'ctx_768', 'L0_xattn_ln1_g', 'L0_xattn_ln1_b', 'L0_xattn_ln2_g', 'L0_xattn_ln2_b', 'L0_xattn_Wq',
        'L0_xattn_bq', 'L0_xattn_Wk', 'L0_xattn_bk', 'L0_xattn_Wv', 'L0_xattn_bv', 'L0_xattn_Wo', 'L0_xattn_bo',
        'L0_ffn_fast_b', 'L0_ffn_w_fc', 'L0_ffn_w_proj', 'L0_ffn_u', 'L0_ffn_v', 'L0_ffn_gate']
_OUTS = [((16, 256, 512), 'float32')]


def kernel(**inputs):
    import numpy as _np
    import concourse.bacc as _bacc
    from concourse import mybir as _mybir
    from concourse.bass_utils import run_bass_kernel_spmd as _run

    nc = _bacc.Bacc("TRN2", target_bir_lowering=False, num_devices=1, dynamic_dma_scratch_size=1024)
    arrays, args = {}, []
    for name in _INS:
        a = _np.ascontiguousarray(inputs[name])
        arrays[f"in_{name}_dram"] = a
        args.append(nc.dram_tensor(f"in_{name}_dram", a.shape, _mybir.dt.from_np(a.dtype), kind="ExternalInput").ap())
    for i, (shape, dtype) in enumerate(_OUTS):
        dt = _mybir.dt.from_np(_np.dtype(dtype))
        args.append(nc.dram_tensor(f"out_{i}_dram", shape, dt, kind="ExternalOutput").ap())
    mk_xattn_ffn(nc, *args)
    r = _run(nc, [arrays], core_ids=[0])
    got = tuple(r.results[0][f"out_{i}_dram"] for i in range(len(_OUTS)))
    return got[0]
```

```python
from contextlib import ExitStack

import concourse.bass as bass
from concourse import mybir

P = 128
ALU = mybir.AluOpType
ACT = mybir.ActivationFunctionType
F32 = mybir.dt.float32
F32R = mybir.dt.float32r
BF16 = mybir.dt.bfloat16
AX_X = mybir.AxisListType.X
HI, LO = 0, 1
EPS = 1e-5

TILES = 4
TOK = TILES * P
NFF = 16
PIECES = 2 * NFF
DVE_STORES = (3,)

ATTENTION = ([("n1T", t) for t in range(4)] + [("n2T", t) for t in range(4)]
             + [("t", 0), ("t", 1), ("t", 2), ("s", 0), ("s", 1), ("s", 2), ("pT", 0), ("s", 3), ("pT", 1),
                ("w", 0), ("w", 1), ("w", 2), ("a", 0), ("a", 1), ("a", 2), ("a", 3)])
BODY = [("x", 0), ("x", 1), ("x", 2), ("x", 3), ("L", 0)] + ATTENTION


def unit_list(b):
    return ATTENTION if isinstance(b, int) and b < 0 else BODY


def units_before(b, kept):
    if isinstance(b, int) and b < 0:
        return 0
    return b * sum(map(kept, BODY)) + sum(map(kept, ATTENTION))


def count(b, unit, kept=lambda u: True):
    seq = unit_list(b)
    return units_before(b, kept) + sum(map(kept, seq[:seq.index(unit) + 1]))


def on_act(unit):
    return unit[0] != "a"


def n_full(b, unit):
    return count(b, unit)


def n_act(b, unit):
    return count(b, unit, on_act)


def n_dve(b, unit):
    return count(b, unit)


def bank_of(b, unit):
    if unit == ("x", 2):
        return "H0"
    if unit == ("x", 3):
        return "H1"
    n = unit_list(b).index(unit)
    if unit_list(b) is ATTENTION and n >= 8:
        return ("G0", "H0", "G1", "H1")[n % 4]
    return f"G{(n if n < 4 else n + 1) % 2}"


def bank_before(b, unit):
    seq, bank = unit_list(b), bank_of(b, unit)
    for u in reversed(seq[:seq.index(unit)]):
        if bank_of(b, u) == bank:
            return b, u
    if isinstance(b, int) and b < 0:
        return None
    for u in reversed(unit_list(b - 1)):
        if bank_of(b - 1, u) == bank:
            return b - 1, u


BODY_TABLE = [
    ("nc0", 4, 3, 3), ("nx0", 4, 3, 4), ("nx1", 5, 5, 5), (("n1T", 0), 7, 7, 8), ("nc1", 7, 7, 8),
    (("n1T", 1), 7, 7, 8), ("nx2", 9, 9, 9), ("nc2", 9, 10, 11), ("nc3", 9, 10, 11), ("nx3", 11, 11, 12),
    (("n1T", 2), 11, 11, 12), (("n1T", 3), 13, 12, 13), (("n2T", 0), 13, 13, 14), (("n2T", 1), 14, 13, 14),
    (("n2T", 2), 15, 13, 14), (("n2T", 3), 15, 13, 16), ("residual", 16, 15, 17), (("t", 0), 17, 17, 17),
    (("t", 1), 17, 17, 17), (("t", 2), 17, 17, 17), (("s", 0), 18, 17, 17), (("n2", 0), 18, 18, 17),
    (("s", 1), 18, 18, 18), (("n2", 1), 18, 18, 18), (("s", 2), 19, 18, 19), (("n2", 2), 20, 18, 19),
    (("pT", 0), 20, 19, 20), (("n2", 3), 21, 20, 20), (("s", 3), 21, 20, 20), ("xs01+", 22, 22, 21),
    (("pT", 1), 23, 22, 22), ("xs23+", 23, 22, 23), (("w", 0), 24, 22, 23), (("w", 1), 24, 22, 23),
    (("w", 2), 25, 23, 24), ("cs01+", 26, 24, 25), ("cs23+", 26, 24, 26), (("a", 0), 26, 24, 27),
    (("a", 1), 26, 24, 27), ("nX1", 26, 24, 27), ("nX0", 27, 25, 27), (("a", 2), 27, 27, 27),
    (("a", 3), 27, 29, 27),
]


def placed(engine, h):
    column = {"pe": 1, "act": 2, "dve": 3, "pool": 3}[engine]
    return [row[0] for row in BODY_TABLE if row[column] == h]


def body_steps(attention, leftover, engine):
    out = ["nX2", ("x", 0), "nX3", ("x", 1)] if engine == "dve" else [("x", 0), ("x", 1)]
    if leftover:
        out += [("down-", NFF - 2)]
    out += [("x", 2), ("x", 3)]
    if leftover:
        out += [("down-", NFF - 1), "out01"]
    else:
        out += ["xs01", "xs23", "cs01", "cs23"]
    out += [("L", 0)]
    if leftover:
        out += ["out23"]
    for j in range(NFF):
        out += [("up", j)]
        out += placed(engine, 2 * j) if attention else []
        out += [("sq", j), ("hi", j)]
        if j >= 2:
            out += [("down", j - 2)]
        out += placed(engine, 2 * j + 1) if attention else []
        out += [("lo", j)]
    return out


def piece_steps():
    out = [("abs", k) for k in range(4)] + [("scale", 0), ("sides", 0)] + [("abs", k) for k in (4, 5)]
    for j in range(PIECES + 3):
        if j % 4 == 3 and j // 4 + 1 < 8:
            out += [("scale", j // 4 + 1)]
        if j + 1 < PIECES:
            out += [("sides", j + 1)]
        if j < PIECES:
            out += [("tern", j)]
        if 1 <= j <= PIECES:
            out += [("turn", j - 1)]
        if j >= 3:
            out += [("store", j - 3)]
        if j < 2 or 3 <= j <= PIECES - 6:
            out += [("abs", j + 6 if j < 2 else j + 5)]
        if j == 18:
            out += ["uprep"]
        if j in (22, 23, 24, 25):
            out += [("ut", j - 22)]
        if j == 30:
            out += ["diag"]
        if j == 32:
            out += ["sprow"]
        if j == 34:
            out += ["sprow_out"]
    return out


def prologue_steps(engine):
    column = {"pe": 1, "act": 2, "dve": 3, "pool": 4}[engine]
    pieces = piece_steps()
    out, done = [], 0
    for row in PROLOGUE_TABLE:
        step = ("job", JOBS.index(row[0])) if row[0] in JOBS else row[0]
        out += pieces[done:row[column]] + [step]
        done = max(done, row[column])
    return out + pieces[done:]


PROLOGUE_TABLE = [
    (("wqT", 0), 0, 0, 1, 1), (("wqT", 1), 0, 0, 2, 2), (("wqT", 2), 0, 0, 2, 2), (("wqT", 3), 0, 0, 3, 4),
    ("b1rep", 2, 0, 3, 5), ("gainK", 2, 0, 3, 5), (("bq", 0), 8, 0, 3, 5), (("wkT", 0), 8, 2, 3, 6),
    (("wkT", 1), 8, 4, 7, 7), (("wkT", 2), 10, 7, 11, 9), ("xs01", 10, 8, 12, 9), ("xs23", 11, 15, 14, 12),
    (("M", 0), 12, 16, 14, 16), ("cs01", 12, 25, 15, 20), ("nx0", 12, 25, 20, 23), ("nx1", 12, 32, 28, 29),
    ("cs23", 18, 32, 31, 32), ("nc0", 21, 32, 31, 32), ("nc1", 26, 32, 39, 34), ("nc2", 31, 37, 42, 38),
    (("M", 1), 33, 39, 43, 40), (("M", 2), 35, 40, 46, 44), ("tb", 35, 40, 46, 45), ("nc3", 35, 40, 46, 53),
    (("n1T", 0), 35, 40, 46, 54), ("nx2", 35, 40, 46, 55), ("nx3", 35, 40, 46, 55), (("M", 3), 35, 40, 46, 55),
    (("n1T", 1), 35, 40, 46, 55), (("wvT", 0), 39, 41, 50, 62), (("n1T", 2), 39, 41, 50, 63),
    (("wvT", 1), 39, 45, 50, 65), (("n1T", 3), 42, 47, 51, 67), (("wvT", 2), 48, 48, 56, 67),
    (("bv", 0), 48, 55, 60, 75), (("wvo", 0), 63, 73, 74, 76), (("n2T", 0), 73, 85, 87, 94),
    (("n2T", 1), 79, 89, 94, 104), (("wvo", 1), 79, 92, 94, 107), (("n2T", 2), 96, 93, 99, 109),
    (("wvo", 2), 96, 93, 103, 124), (("n2T", 3), 102, 97, 111, 141), (("co", 0), 104, 101, 118, 141),
    (("fb", 0), 104, 112, 118, 141), (("t", 0), 117, 117, 122, 141), (("t", 1), 124, 126, 124, 141),
    (("t", 2), 125, 130, 130, 141), ("residual", 131, 133, 132, 143), (("s", 0), 133, 133, 133, 143),
    (("n2", 0), 133, 135, 139, 143), (("s", 1), 133, 140, 144, 143), (("n2", 1), 133, 141, 144, 143),
    (("s", 2), 133, 157, 149, 145), (("n2", 2), 135, 157, 155, 152), (("pT", 0), 143, 158, 160, 156),
    (("n2", 3), 159, 169, 167, 157), (("s", 3), 159, 171, 169, 168), (("pT", 1), 174, 179, 172, 179),
    (("w", 0), 176, 181, 182, 186), (("w", 1), 179, 192, 183, 196), (("w", 2), 197, 203, 199, 213),
    (("a", 0), 204, 209, 203, 216), (("a", 1), 204, 213, 207, 217), ("nX0", 208, 222, 213, 222),
    (("a", 2), 208, 227, 213, 237), ("nX1", 208, 227, 213, 237), (("a", 3), 220, 234, 227, 243),
]

JOBS = ([("wqT", c) for c in range(4)] + [("bq", 0)] + [("wkT", c) for c in range(3)]
        + [("M", c) for c in range(4)] + [("wvT", c) for c in range(3)] + [("bv", 0)]
        + [("wvo", c) for c in range(3)] + [("co", 0), ("fb", 0)])


def mk_xattn_ffn(nc, x, ctx_768, ln1_g, ln1_b, ln2_g, ln2_b, Wq, bq, Wk, bk, Wv, bv, Wo, bo,
                 fast_b, w_fc, w_proj, u, v, gate, out):
    NB, S, D = x.shape
    DC = ctx_768.shape[2]
    E = Wq.shape[1]
    HID = w_fc.shape[0]
    RK = fast_b.shape[0]
    KD, KC, KE = D // P, DC // P, E // P
    NG = NB * S // TOK
    assert S == 256 and D == 512 and E == 512 and HID == NFF * P and RK == 16 and NG == 8
    SM = float(E) ** -0.5

    x_in = x.rearrange("(g c) (p t) d -> g p c (t d)", c=2, t=2)
    ctx_in = ctx_768.rearrange("(g c) (p t) d -> g p c (t d)", c=2, t=2)
    out_v = out.rearrange("(g c) (p t) d -> g c p (t d)", c=2, t=2)

    with ExitStack() as stack:
        def sb(name, shape, dt=F32, where=stack):
            return where.enter_context(nc.sbuf_tensor(name, shape, dt))

        def sem(name):
            return stack.enter_context(nc.semaphore(name))

        fcT = sb("fcT", [P, KD, HID], F32R)
        projT = sb("projT", [P, NFF, D], F32R)
        M = sb("M", [P, 2, KD, DC], F32R)
        Wvo = sb("Wvo", [P, 2, KC, D], F32R)
        uT = sb("uT", [P, HID], F32R)
        FB = sb("FB", [P, KD, P], F32R)
        ident = sb("ident", [P, P])
        identb = sb("identb", [P, P], BF16)
        sprow = sb("sprow", [P, D])
        crow = sb("crow", [P, D])
        bqrow = crow[:, :]
        tbias = sb("tbias", [P, KC])
        scf = sb("scf", [P, NFF])
        half = sb("half", [P, 2, 4])
        spc = sb("spc", [P, KD])
        asum = sb("asum", [P, 8, 4])
        psum4 = sb("proj_row_sums", [P, 4])
        urs = sb("urs", [P, NFF])
        g1c = sb("g1c", [P, KD])
        b1c = sb("b1c", [P, KD])
        g2c = sb("g2c", [P, KC])
        b2c = sb("b2c", [P, KC])
        bvc = sb("bvc", [P, KE])
        bvp = sb("bvp", [P, KE])
        gatec = sb("gatec", [P, 1])
        xst = sb("xst", [P, TILES, 6])
        xmv = sb("xmv", [P, TILES, 2])
        xrs = sb("xrs", [P, TILES])
        cst = sb("cst", [P, TILES, 6])
        cmv = sb("cmv", [P, TILES, 2])
        crs = sb("crs", [P, TILES])
        mhalf = sb("mhalf", [P, TILES])
        spare = sb("spare", [P, 1])
        nst = sb("nst", [P, TILES, 6])
        nmv = sb("nmv", [P, TILES, 2])
        nrs = sb("nrs", [P, TILES])
        rowmax = sb("rowmax", [P, TILES])
        nmax = sb("nmax", [P, TILES])
        rowsum = sb("rowsum", [P, TILES])
        rinv = sb("rinv", [P, TILES])
        ctxb = sb("ctxb", [P, TILES, DC])
        xb = sb("xb", [P, TILES, D])
        pbuf = sb("pbuf", [P, TILES, S])
        nrm = sb("nrm", [P, 2, D])
        tstack = sb("tstack", [P, TOK], F32R)
        x2a = sb("x2a", [P, TILES, D])
        ybuf = [pbuf[:, 2 * t:2 * t + 2, :].rearrange("p a s -> p (a s)") for t in range(2)] + [
            nrm[:, t, :] for t in range(2)]

        setup = ExitStack()
        wring = sb("wring", [P, 2, 4, D], F32, setup)
        Wq_s = sb("Wq_s", [P, KD, E], F32, setup)
        Wk_s = sb("Wk_s", [P, KC, E], F32, setup)
        WqT = sb("WqT", [P, KE, D], F32, setup)
        WkT = sb("WkT", [P, KE, DC], F32, setup)
        Wv_s = sb("Wv_s", [P, KC, E], F32, setup)
        WvT = sb("WvT", [P, KE, DC], F32, setup)
        Wo_s = sb("Wo_s", [P, KE, D], F32, setup)
        tern = sb("tern", [P, 4, D], BF16, setup)
        unat = sb("unat", [P, NFF, 8, RK], F32, setup)
        ones = sb("ones", [P, P], F32, setup)
        bvrep = sb("bvrep", [P, KE, P], F32, setup)
        above = sb("above", [P, 2, D], BF16, setup)
        below = sb("below", [P, 2, D], BF16, setup)
        absj = sb("absj", [P, 2, D], BF16, setup)
        u_s = sb("u_s", [P, NFF, RK], F32, setup)
        fbT4 = sb("fbT4", [RK, 4, RK], F32, setup)
        uhi = sb("uhi", [P, NFF, RK], F32R, setup)
        setup.close()
        xnT = sb("xnT", [P, 2, KD, TOK], F32R)
        n1T = sb("n1T", [P, 2, KD, TOK], F32R)
        n2T = sb("n2T", [P, 2, KC, TOK], F32R)
        tT = sb("tT", [P, 2, KC, TOK], F32R)
        pT = sb("pT", [P, 2, 2, 2, S], F32R)
        rbuf = sb("rbuf", [P, 2, TOK])
        x2b = sb("x2b", [P, TILES, D])
        qbuf = sb("qbuf", [P, 2, 2, TOK], F32R)
        n2rows = n1T
        x2 = [x2a, x2b]
        v_s = pbuf[0:RK, 0:2, :].rearrange("p a b -> p (a b)")
        borow = pbuf[:, 2:4, :].rearrange("p a b -> p (a b)")

        banks = {n: stack.enter_context(nc.psum_tensor(n, [P, 512], F32))
                 for n in ("G0", "G1", "H0", "H1", "O0", "O1", "O2", "O3")}

        gains_in, lowrank_in = sem("gains_in"), sem("lowrank_in")
        b1_in, bq_in, vbias_in = sem("b1_in"), sem("bq_in"), sem("v_biases_in")
        gained = sem("Wk_gained")
        sides_made = sem("sides_made")
        sprow_made = sem("sprow_made")
        wq_in = [sem(f"wq{c}_in") for c in range(KD)]
        wk_in, wv_in, wo_in = sem("wk_in"), sem("wv_in"), sem("wo_in")
        x_in_s, ctx_in_s = sem("x_loaded"), sem("ctx_loaded")
        ring_in = [sem(f"ring{i}_in") for i in range(8)]
        stored = sem("stored")
        ident_made, identb_made, ones_made = sem("ident_made"), sem("identb_made"), sem("ones_made")
        b1rep_made = sem("b1rep_made")
        tb_products, tb_made = sem("tbias_products"), sem("tbias_made")
        job_full = sem("job_full")
        job_act = sem("job_act")
        job_dve = sem("job_dve")
        own = sem("dve_chain")
        pool_own = sem("pool_chain")
        abs_done = sem("abs_done")
        scales_made = sem("scales_made")
        tern_made = sem("tern_made")
        tern_turned = sem("tern_turned")
        act_stored, dve_stored = sem("pieces_stored_by_ScalarE"), sem("pieces_stored_by_VectorE")
        unat_made = sem("unat_made")
        ut_full = sem("ut_full")
        ut_stored = sem("ut_stored")
        diag_made = sem("diag_made")
        sprow_full = sem("sprow_full")
        unit_full = sem("unit_full")
        unit_act = sem("unit_act")
        unit_dve = sem("unit_dve")
        var_made = sem("var_made")
        rstd_made = sem("rstd_made")
        in_var_made, in_rstd_made = sem("inputs_var_made"), sem("inputs_rstd_made")
        n1_made = sem("n1_made")
        n2_made = sem("n2_made")
        n2hi_made, n2lo_made = sem("n2_hi_made"), sem("n2_lo_made")
        xn_made = sem("xn_made")
        res_made = sem("residual_made")
        up_full = sem("up_full")
        relu_made = sem("relu_made")
        square_made = sem("square_made")
        sqhi_made = sem("square_hi_made")
        sqlo_made = sem("square_lo_made")
        down_full = sem("down_full")
        y_made = sem("y_made")
        y_added = sem("y_added")
        odd_y_added = sem("last_odd_y_added")

        def job_engines(n):
            kind = JOBS[n][0]
            if n < 2:
                return ("dve",)
            if kind == "wvT":
                return ("act",)
            if kind in ("wqT", "wkT"):
                return ("act",) if n % 2 == 0 else ("dve",)
            return ("act", "dve") if kind in ("M", "wvo", "fb") else ("dve",)

        def job_count(n, engine):
            return sum(engine in job_engines(i) for i in range(n + 1))

        def job_read(e, n):
            last = job_engines(n)[-1]
            e.wait_ge(job_act if last == "act" else job_dve, job_count(n, last))

        def run_bodies(e, steps, engine):
            steps(-1, prologue_steps(engine))
            steps(0, body_steps(True, False, engine))
            with e.Fori(0, (NG - 2) // 2) as pair:
                for odd in (1, 0):
                    steps(2 * pair + 2 - odd, body_steps(True, True, engine), odd)
            steps(NG - 1, body_steps(False, True, engine))

        block = stack.enter_context(nc.Block())

        FBp = FB[:, :, :].rearrange("p k (a h n) -> p k a h n", a=2, h=2)

        def fb_of(bank):
            return bank[:, 0:KD * 64].rearrange("p (k a n) -> p k a n", k=KD, a=2)

        def piece_place(j):
            if j < NFF:
                return fcT[:, :, j * P:(j + 1) * P]
            t, q = (j - NFF) // 4, (j - NFF) % 4
            return projT[:, 4 * q:4 * q + 4, t * P:(t + 1) * P]

        def piece_stored(e, j):
            mine = j % 4 in DVE_STORES
            e.wait_ge(dve_stored if mine else act_stored,
                      sum((i % 4 in DVE_STORES) == mine for i in range(j + 1)))

        def piece_bank(j):
            return banks[f"O{j % 4}"][:, 0:256].bitcast(BF16).rearrange("p (k n) -> p k n", k=4)

        def columns(e, dst, src, to):
            e.dma_start(dst[:, :], src.rearrange("(c p) -> p c", p=P), allow_slow_non_contiguous=True
                        ).then_inc(to, 16)

        @block.sync
        def _(sp):
            for c in range(KD):
                sp.dma_start(Wq_s[:, c, :], Wq[c * P:(c + 1) * P, :]).then_inc(wq_in[c], 16)

            def ring_load(k):
                src = (w_fc.rearrange("(k p) d -> k p d", p=P)[k] if k < NFF
                       else w_proj.rearrange("(t p) (c d) -> t p c d", p=P, d=D)[(k - NFF) // 4][:, k % 4, :])
                sp.dma_start(wring[:, k // 4 % 2, k % 4, :], src).then_inc(ring_in[k % 8], 16)

            def load_next(b):
                sp.wait_ge(n1_made, 4 * (b + 2))
                sp.wait_ge(res_made, 4 * (b + 2))
                sp.dma_start(xb[:, :, :].rearrange("p (c t) d -> p c (t d)", c=2), x_in[b + 2]).then_inc(x_in_s, 16)
                sp.wait_ge(unit_full, n_full(b, ("n2T", 3)))
                sp.wait_ge(n2lo_made, 4 * (b + 2))
                sp.dma_start(ctxb[:, :, :].rearrange("p (c t) d -> p c (t d)", c=2), ctx_in[b + 2]
                             ).then_inc(ctx_in_s, 16)

            def store(g, tiles_of):
                for c in range(2):
                    sp.wait_ge(y_added, 4 * g + 2 * c + 2)
                    sp.dma_start(out_v[g, c], x2[tiles_of][:, 2 * c:2 * c + 2, :].rearrange("p t d -> p (t d)")
                                 ).then_inc(stored, 16)

            sp.dma_start(Wk_s[:, :, :], Wk.rearrange("(c p) e -> p c e", p=P)).then_inc(wk_in, 16)
            for k in range(4):
                ring_load(k)
            sp.dma_start(bqrow, bq.partition_broadcast(P)).then_inc(bq_in, 16)
            sp.dma_start(xb[:, :, :].rearrange("p (c t) d -> p c (t d)", c=2), x_in[0]).then_inc(x_in_s, 16)
            for k in range(4, 8):
                ring_load(k)
            sp.dma_start(ctxb[:, :, :].rearrange("p (c t) d -> p c (t d)", c=2), ctx_in[0]).then_inc(ctx_in_s, 16)
            sp.dma_start(Wv_s[:, :, :], Wv.rearrange("(c p) e -> p c e", p=P)).then_inc(wv_in, 16)
            sp.dma_start(Wo_s[:, :, :], Wo.rearrange("(c p) e -> p c e", p=P)).then_inc(wo_in, 16)
            columns(sp, b2c, ln2_b, vbias_in)
            columns(sp, bvc, bv, vbias_in)
            sp.dma_start(borow, bo.partition_broadcast(P)).then_inc(vbias_in, 16)
            sp.dma_start(gatec[:, :], gate.partition_broadcast(P)).then_inc(lowrank_in, 16)
            sp.dma_start(v_s, v).then_inc(lowrank_in, 16)
            for i in range(4):
                sp.dma_start(fbT4[:, i, :], fast_b.rearrange("r s -> s r"), allow_slow_non_contiguous=True
                             ).then_inc(lowrank_in, 16)
            sp.dma_start(u_s[:, :, :], u.rearrange("(c p) r -> p c r", p=P)).then_inc(lowrank_in, 16)
            for k in range(8, PIECES):
                sp.wait_ge(sides_made, k - 7)
                ring_load(k)
            load_next(-1)
            load_next(0)
            with sp.Fori(0, 2) as pair:
                for odd in (1, 0):
                    store(2 * pair + 1 - odd, 1 - odd)
                    load_next(2 * pair + 2 - odd)
            store(4, 0)
            load_next(5)
            store(5, 1)
            sp.wait_ge(n1_made, 4 * NG)
            sp.wait_ge(res_made, 4 * NG)
            sp.dma_start(xb[0:1, 0:2, :].rearrange("p t d -> p (t d)"), x_in[NG - 1][0:1, 0, :]).then_inc(x_in_s, 16)
            sp.wait_ge(unit_full, n_full(NG - 2, ("n2T", 3)))
            sp.wait_ge(n2lo_made, 4 * NG)
            sp.dma_start(ctxb[0:1, 0:2, :].rearrange("p t d -> p (t d)"), ctx_in[NG - 1][0:1, 0, :]
                         ).then_inc(ctx_in_s, 16)
            store(6, 0)
            for t in range(TILES):
                if t % 2:
                    sp.wait_ge(odd_y_added, t // 2 + 1)
                else:
                    sp.wait_ge(y_added, 4 * (NG - 1) + t // 2 + 1)
                sp.dma_start(out_v[NG - 1, t // 2][:, t % 2 * D:(t % 2 + 1) * D], x2[1][:, t, :]).then_inc(stored, 16)
            sp.wait_ge(stored, 32 * (NG - 1) + 16 * TILES)

        @block.gpsimd
        def _(pool):
            nc.gpsimd.memset(ident[:, :], 0.0).then_inc(pool_own, 1)
            pool.wait_ge(pool_own, 1)
            nc.gpsimd.affine_select(out=ident[:, :], in_=ident[:, :], compare_op=ALU.not_equal, fill=1.0, base=0,
                                    pattern=[[-1, P]], channel_multiplier=1).then_inc(ident_made, 1)
            nc.gpsimd.memset(ones[:, :], 1.0).then_inc(ones_made, 1)
            nc.gpsimd.memset(mhalf[:, :], -0.5).then_inc(pool_own, 1)
            pool.wait_ge(ident_made, 1)
            nc.gpsimd.tensor_copy(identb[:, :], ident[:, :]).then_inc(identb_made, 1)
            pool.wait_ge(pool_own, 2)

            def steps(b, todo, odd=None):
                g = b + 1
                par = 0 if isinstance(b, int) and b < 0 else (odd + 1) % 2 if odd is not None else (b + 1) % 2
                for st in todo:
                    roots = {"xs23": (0, xrs[:, :]), "cs23": (1, crs[:, :]), "xs23+": (2, xrs[:, :]),
                             "cs23+": (3, crs[:, :])}
                    if st[0] == "tern":
                        j = st[1]
                        if j >= 4:
                            pool.wait_ge(tern_turned, j - 3)
                        pool.wait_ge(sides_made, j + 1)
                        nc.gpsimd.tensor_tensor(tern[:, j % 4, :], above[:, j % 2, :], below[:, j % 2, :],
                                                ALU.subtract).then_inc(tern_made, 1)
                    elif st in roots:
                        n, var = roots[st]
                        pool.wait_ge(in_var_made, 2 * g + n + 1)
                        nc.gpsimd.tensor_tensor(var, var, mhalf[:, :], ALU.pow).then_inc(in_rstd_made, 1)
                    elif st[0] == "a":
                        t = st[1]
                        pool.wait_ge(var_made, TILES * g + t + 1)
                        nc.gpsimd.tensor_tensor(nrs[:, t:t + 1], nrs[:, t:t + 1], mhalf[:, 0:1], ALU.pow
                                                ).then_inc(rstd_made, 1)
                    elif st == "tb":
                        pool.wait_ge(job_dve, job_count(JOBS.index(("bq", 0)), "dve"))
                        for m in range(KC):
                            nc.gpsimd.tensor_tensor(x2a[:, m, :], Wk_s[:, m, :], x2a[:, KC, :], ALU.mult
                                                    ).then_inc(tb_products, 1)
                    elif st == "residual":
                        pool.wait_ge(x_in_s, 16 * (g + 1))
                        if isinstance(b, int) and b < 0:
                            pool.wait_ge(job_dve, job_count(JOBS.index(("co", 0)), "dve"))
                            pool.wait_ge(tb_made, KC)
                        elif isinstance(b, int) and b == 0:
                            pool.wait_ge(ut_full, 4)
                        else:
                            pool.wait_ge(stored, 32 * b)
                        for t in range(TILES):
                            nc.gpsimd.tensor_tensor(x2[par][:, t, :], xb[:, t, :], crow[:, :],
                                                    ALU.add).then_inc(res_made, 1)
                    elif st == "out23":
                        for t in range(TILES):
                            pool.wait_ge(y_made, 4 * (b - 1) + t + 1)
                            nc.gpsimd.tensor_tensor(x2[par][:, t, :], x2[par][:, t, :], ybuf[t],
                                                    ALU.add).then_inc(y_added, 1)
            run_bodies(pool, steps, "pool")
            for t in (0, 2):
                pool.wait_ge(y_made, 4 * (NG - 1) + t + 1)
                nc.gpsimd.tensor_tensor(x2[1][:, t, :], x2[1][:, t, :], ybuf[t], ALU.add).then_inc(y_added, 1)

        @block.scalar
        def _(act):
            columns(act, g2c, ln2_g, gains_in)
            columns(act, g1c, ln1_g, gains_in)
            columns(act, b1c, ln1_b, b1_in)

            def job(n):
                kind, c = JOBS[n]
                if "act" not in job_engines(n):
                    return
                bank = banks[f"H{n % 2}"]
                act.wait_ge(job_full, n + 1)
                if kind == "wqT":
                    nc.scalar.activation(WqT[:, :, c * P:(c + 1) * P], bank[:, :].rearrange("p (k n) -> p k n", k=KE),
                                         ACT.Copy).then_inc(job_act, 1)
                elif kind == "wkT":
                    nc.scalar.activation(WkT[:, :, c * P:(c + 1) * P], bank[:, :].rearrange("p (k n) -> p k n", k=KE),
                                         ACT.Copy).then_inc(job_act, 1)
                elif kind == "wvT":
                    nc.scalar.activation(WvT[:, :, c * P:(c + 1) * P], bank[:, :].rearrange("p (k n) -> p k n", k=KE),
                                         ACT.Copy).then_inc(job_act, 1)
                elif kind == "M":
                    act.wait_ge(gains_in, 32)
                    nc.scalar.activation(M[:, HI, c, :], bank[:, 0:DC], ACT.Copy, scale=g1c[:, c:c + 1]
                                         ).then_inc(job_act, 1)
                elif kind == "wvo":
                    nc.scalar.activation(Wvo[:, HI, c, :], bank[:, :], ACT.Copy, scale=g2c[:, c:c + 1]
                                         ).then_inc(job_act, 1)
                elif kind == "fb":
                    nc.scalar.activation(FBp[:, :, :, HI, :], fb_of(bank), ACT.Copy).then_inc(job_act, 1)

            def unit(b, un):
                kind, t = un
                if kind == "a":
                    return
                bank = banks[bank_of(b, un)]
                wide = bank[:, :].rearrange("p (k n) -> p k n", k=4)
                cols = slice(t * P, (t + 1) * P)
                if kind == "s":
                    if un == ("s", 0) and not (isinstance(b, int) and b <= 0):
                        act.wait_ge(y_added, 4 * b)
                    act.wait_ge(unit_dve, n_dve(b, un))
                    nc.scalar.activation(pbuf[:, t, :], bank[:, 0:S], ACT.Exp, bias=nmax[:, t:t + 1], scale=SM,
                                         accum_out=rowsum[:, t:t + 1]).then_inc(unit_act, 1)
                    return
                act.wait_ge(unit_full, n_full(b, un))
                if kind == "x":
                    if isinstance(b, int) and b == 0 and t == 0:
                        act.wait_ge(tern_made, PIECES)
                    nc.scalar.activation(xnT[:, HI, :, cols], wide, ACT.Copy).then_inc(unit_act, 1)
                elif kind == "L":
                    nc.scalar.activation(tstack[:, :], bank[:, :], ACT.Copy).then_inc(unit_act, 1)
                elif kind == "n1T":
                    if isinstance(b, int) and b < 0 and t == 0:
                        act.wait_ge(tb_products, KC)
                    nc.scalar.activation(n1T[:, HI, :, cols], wide, ACT.Copy).then_inc(unit_act, 1)
                elif kind == "n2T":
                    nc.scalar.activation(n2T[:, HI, :, cols], wide[:, 0:KC, :], ACT.Copy).then_inc(unit_act, 1)
                elif kind == "t":
                    if isinstance(b, int) and b < 0 and t == 0:
                        act.wait_ge(tb_made, KC)
                    nc.scalar.activation(tT[:, HI, t, :], bank[:, :], ACT.Identity, bias=tbias[:, t:t + 1]
                                         ).then_inc(unit_act, 1)
                elif kind == "w":
                    nc.scalar.activation(tT[:, HI, t, :], bank[:, :], ACT.Copy).then_inc(unit_act, 1)
                elif kind == "pT":
                    nc.scalar.activation(pT[:, HI, t, :, :], bank[:, :].rearrange("p (j q) -> p j q", j=2),
                                         ACT.Copy).then_inc(unit_act, 1)

            def steps(b, todo, odd=None):
                for st in todo:
                    kind, j = st if isinstance(st, tuple) else (st, None)
                    if kind in ("x", "L", "n1T", "n2T", "t", "s", "w", "pT", "a"):
                        unit(b, st)
                    elif kind == "up":
                        act.wait_ge(up_full, NFF * b + j + 1)
                        if not (isinstance(b, int) and b == 0 and j < 2):
                            act.wait_ge(sqlo_made, NFF * b + j - 1)
                        nc.scalar.activation(rbuf[:, j % 2, :], banks[f"H{j % 2}"][:, :], ACT.Relu,
                                             scale=scf[:, j:j + 1]).then_inc(relu_made, 1)
                    elif kind == "hi":
                        act.wait_ge(square_made, NFF * b + j + 1)
                        if not (isinstance(b, int) and b == 0 and j < 2):
                            act.wait_ge(down_full, NFF * b + j - 1)
                        nc.scalar.activation(qbuf[:, j % 2, HI, :], rbuf[:, j % 2, :], ACT.Copy
                                             ).then_inc(sqhi_made, 1)
                    elif kind == "n2":
                        if j == 0:
                            act.wait_ge(unit_full, n_full(b, ("t", 2)))
                        act.wait_ge(n2_made, 4 * (b + 1) + j + 1)
                        nc.scalar.activation(n2rows[:, HI, j, 0:DC], ctxb[:, j, :], ACT.Copy).then_inc(n2hi_made, 1)
                    elif kind == "job":
                        job(j)
                    elif kind == "tb":
                        for m in range(KC):
                            act.wait_ge(tb_products, m + 1)
                            nc.scalar.activation(x2a[:, m, :], x2a[:, m, :], ACT.Copy, accum_out=tbias[:, m:m + 1]
                                                 ).then_inc(tb_made, 1)
                    elif kind == "abs":
                        act.wait_ge(ring_in[j % 8], 16 * (j // 8 + 1))
                        if j >= 2:
                            act.wait_ge(abs_done, j - 1)
                        nc.scalar.activation(absj[:, j % 2, :], wring[:, j // 4 % 2, j % 4, :], ACT.Abs,
                                             accum_out=asum[:, j // 4, j % 4:j % 4 + 1]).then_inc(abs_done, 1)
                    elif kind == "store" and j % 4 not in DVE_STORES:
                        act.wait_ge(tern_turned, j + 1)
                        nc.scalar.activation(piece_place(j), piece_bank(j), ACT.Copy).then_inc(act_stored, 1)
                    elif kind == "ut":
                        act.wait_ge(ut_full, j + 1)
                        nc.scalar.activation(uT[:, j * 512:(j + 1) * 512], banks[f"O{(j + 23) % 4}"][:, :], ACT.Copy
                                             ).then_inc(ut_stored, 1)
            run_bodies(act, steps, "act")

        @block.vector
        def _(dve):
            chain = {"base": 0, "n": 0, "extra": 0}

            def link(ins):
                chain["n"] += 1
                ins.then_inc(own, 1)
                dve.wait_ge(own, chain["base"] + chain["n"])

            def link_to_aggr(ins):
                link(ins)
                nc.vector.memset(spare[:, :], 0.0)

            def job(n):
                kind, c = JOBS[n]
                if "dve" not in job_engines(n):
                    return
                bank = banks[f"H{n % 2}"]
                dve.wait_ge(job_full, n + 1)
                wide = bank[:, :].rearrange("p (k n) -> p k n", k=KE)
                if kind == "wqT":
                    nc.vector.tensor_copy(WqT[:, :, c * P:(c + 1) * P], wide).then_inc(job_dve, 1)
                elif kind == "wkT":
                    nc.vector.tensor_copy(WkT[:, :, c * P:(c + 1) * P], wide).then_inc(job_dve, 1)
                elif kind == "bq":
                    dve.wait_ge(bq_in, 16)
                    nc.vector.tensor_tensor(x2a[:, KC, :], bank[:, :], bqrow, ALU.add).then_inc(job_dve, 1)
                elif kind == "bv":
                    dve.wait_ge(ones_made, 1)
                    dve.wait_ge(vbias_in, 16 * 3)
                    link(nc.vector.tensor_tensor(bvp[:, :], bank[:, 0:KE], bvc[:, :], ALU.add))
                    for k in range(KE):
                        last = nc.vector.tensor_scalar(bvrep[:, k, :], ones[:, :], bvp[:, k:k + 1], None, ALU.mult)
                    last.then_inc(job_dve, 1)
                elif kind == "M":
                    dve.wait_ge(job_act, job_count(n, "act"))
                    nc.vector.scalar_tensor_tensor(out=M[:, LO, c, :], in0=bank[:, 0:DC], scalar=g1c[:, c:c + 1],
                                                   in1=M[:, HI, c, :], op0=ALU.mult, op1=ALU.subtract
                                                   ).then_inc(job_dve, 1)
                elif kind == "wvo":
                    dve.wait_ge(job_act, job_count(n, "act"))
                    nc.vector.scalar_tensor_tensor(out=Wvo[:, LO, c, :], in0=bank[:, :], scalar=g2c[:, c:c + 1],
                                                   in1=Wvo[:, HI, c, :], op0=ALU.mult, op1=ALU.subtract
                                                   ).then_inc(job_dve, 1)
                elif kind == "co":
                    nc.vector.tensor_tensor(crow[:, :], bank[:, :], borow, ALU.add).then_inc(job_dve, 1)
                elif kind == "fb":
                    dve.wait_ge(job_act, job_count(n, "act"))
                    nc.vector.tensor_tensor(FBp[:, :, :, LO, :], fb_of(bank), FBp[:, :, :, HI, :], ALU.subtract
                                            ).then_inc(job_dve, 1)

            def unit(b, un):
                kind, t = un
                bank = banks[bank_of(b, un)]
                wide = bank[:, :].rearrange("p (k n) -> p k n", k=4)
                cols = slice(t * P, (t + 1) * P)
                if kind == "s":
                    dve.wait_ge(unit_full, n_full(b, un))
                    link(nc.vector.tensor_reduce(rowmax[:, t:t + 1], bank[:, 0:S], AX_X, ALU.max))
                    nc.vector.tensor_scalar(nmax[:, t:t + 1], rowmax[:, t:t + 1], -SM, None, ALU.mult
                                            ).then_inc(unit_dve, 1)
                    return
                if kind == "a":
                    dve.wait_ge(unit_full, n_full(b, un))
                    dve.wait_ge(res_made, 4 * (b + 1) + t + 1)
                    here = x2[cur["par"]]
                    nc.vector.scalar_tensor_tensor(out=here[:, t, :], in0=bank[:, :], scalar=rinv[:, t:t + 1],
                                                   in1=here[:, t, :], op0=ALU.mult, op1=ALU.add
                                                   ).then_inc(unit_dve, 1)
                    dve.wait_ge(unit_dve, n_dve(b, un))
                    link_to_aggr(nc.vector.bn_stats(nst[:, t, :], here[:, t, :]))
                    link(nc.vector.bn_aggr(nmv[:, t, :], nst[:, t, :]))
                    nc.vector.tensor_scalar(nrs[:, t:t + 1], nmv[:, t, 1:2], EPS, None, ALU.add).then_inc(var_made, 1)
                    return
                dve.wait_ge(unit_act, n_act(b, un))
                if kind == "x":
                    nc.vector.tensor_tensor(xnT[:, LO, :, cols], wide, xnT[:, HI, :, cols], ALU.subtract
                                            ).then_inc(unit_dve, 1)
                elif kind == "L":
                    nc.vector.tensor_tensor(tstack[64:128, :], bank[64:128, :], tstack[64:128, :], ALU.subtract
                                            ).then_inc(unit_dve, 1)
                elif kind == "n1T":
                    nc.vector.tensor_tensor(n1T[:, LO, :, cols], wide, n1T[:, HI, :, cols], ALU.subtract
                                            ).then_inc(unit_dve, 1)
                elif kind == "n2T":
                    nc.vector.tensor_tensor(n2T[:, LO, :, cols], wide[:, 0:KC, :], n2T[:, HI, :, cols], ALU.subtract
                                            ).then_inc(unit_dve, 1)
                elif kind == "t":
                    nc.vector.scalar_tensor_tensor(out=tT[:, LO, t, :], in0=bank[:, :], scalar=tbias[:, t:t + 1],
                                                   in1=tT[:, HI, t, :], op0=ALU.add, op1=ALU.subtract
                                                   ).then_inc(unit_dve, 1)
                elif kind == "w":
                    nc.vector.tensor_tensor(tT[:, LO, t, :], bank[:, :], tT[:, HI, t, :], ALU.subtract
                                            ).then_inc(unit_dve, 1)
                elif kind == "pT":
                    nc.vector.tensor_tensor(pT[:, LO, t, :, :], bank[:, :].rearrange("p (j q) -> p j q", j=2),
                                            pT[:, HI, t, :, :], ALU.subtract).then_inc(unit_dve, 1)
                    link(nc.vector.reciprocal(rinv[:, 2 * t:2 * t + 2], rowsum[:, 2 * t:2 * t + 2]))

            cur = {"par": 0}

            def evacuate(g, t):
                if isinstance(g, int) and g == NG - 1:
                    dve.wait_ge(down_full, NFF * g + NFF - 2 + t + 1)
                elif t == 0:
                    dve.wait_ge(down_full, NFF * (g + 1))
                if isinstance(g, int) and g == NG - 1:
                    dve.wait_ge(y_added, 4 * g)
                elif t >= 2:
                    dve.wait_ge(unit_full, n_full(g + 1, ("x", t)))
                nc.vector.tensor_tensor(ybuf[t], banks[f"O{t}"][:, :], sprow[:, :], ALU.mult).then_inc(y_made, 1)

            def steps(b, todo, odd=None):
                first = isinstance(b, int) and b < 0
                g = b + 1
                cur["par"] = 0 if first else (odd + 1) % 2 if odd is not None else (b + 1) % 2
                prev = 1 - cur["par"]
                if first:
                    chain["base"] = 0
                    chain["pro"] = None
                else:
                    if chain["pro"] is None:
                        chain["pro"] = chain["n"]
                    else:
                        chain["extra"] = STATISTICS
                    chain["base"] = chain["pro"] + chain["extra"] + PER_BODY * b
                    chain["n"] = 0
                for st in todo:
                    kind, j = st if isinstance(st, tuple) else (st, None)
                    if kind in ("x", "L", "n1T", "n2T", "t", "s", "w", "pT", "a"):
                        unit(b, st)
                    elif kind == "n2":
                        dve.wait_ge(n2hi_made, 4 * (b + 1) + j + 1)
                        nc.vector.tensor_tensor(n2rows[:, LO, j, 0:DC], ctxb[:, j, :], n2rows[:, HI, j, 0:DC],
                                                ALU.subtract).then_inc(n2lo_made, 1)
                    elif kind == "job":
                        job(j)
                    elif kind == "gainK":
                        dve.wait_ge(gains_in, 32)
                        dve.wait_ge(wk_in, 16)
                        for k in range(KC):
                            last = nc.vector.tensor_scalar(Wk_s[:, k, :], Wk_s[:, k, :], g2c[:, k:k + 1], None,
                                                           ALU.mult)
                        last.then_inc(gained, 1)
                    elif kind == "b1rep":
                        dve.wait_ge(ones_made, 1)
                        dve.wait_ge(b1_in, 16)
                        for k in range(KD):
                            last = nc.vector.tensor_scalar(bvrep[:, k, :], ones[:, :], b1c[:, k:k + 1], None, ALU.mult)
                        last.then_inc(b1rep_made, 1)
                    elif kind[:2] in ("xs", "cs"):
                        what, part = kind[0], kind[2:4]
                        src, stats, means, var, loaded = ((xb, xst, xmv, xrs, x_in_s) if what == "x" else
                                                          (ctxb, cst, cmv, crs, ctx_in_s))
                        if part == "01":
                            dve.wait_ge(loaded, 16 * (g + (2 if kind[-1] == "+" else 1)))
                        for t in (0, 1) if part == "01" else (2, 3):
                            last = nc.vector.bn_stats(stats[:, t, :], src[:, t, :])
                        if part == "23":
                            link_to_aggr(last)
                            for t in range(TILES):
                                last = nc.vector.bn_aggr(means[:, t, :], stats[:, t, :])
                            link(last)
                            scale, shift = (1.0 + EPS, EPS * EPS) if what == "x" else (1.0, EPS)
                            nc.vector.tensor_scalar(var[:, :], means[:, :, 1], scale, shift, ALU.mult, ALU.add
                                                    ).then_inc(in_var_made, 1)
                    elif kind[:2] == "nx":
                        t = int(kind[2])
                        if t >= 2:
                            dve.wait_ge(unit_full, n_full(b, ("n1T", t - 2)))
                        elif isinstance(b, int) and b == 0:
                            dve.wait_ge(unit_full, n_full(b, ("x", t + 2)))
                        elif not first:
                            dve.wait_ge(y_added, 4 * b)
                        if t == 0:
                            dve.wait_ge(in_rstd_made, 2 * g + 1)
                        nc.vector.tensor_scalar(nrm[:, t % 2, :], xb[:, t, :], xmv[:, t, 0:1], xrs[:, t:t + 1],
                                                ALU.subtract, ALU.mult).then_inc(n1_made, 1)
                    elif kind[:2] == "nc":
                        t = int(kind[2])
                        if t == 0:
                            dve.wait_ge(in_rstd_made, 2 * g + 2)
                        nc.vector.tensor_scalar(ctxb[:, t, :], ctxb[:, t, :], cmv[:, t, 0:1], crs[:, t:t + 1],
                                                ALU.subtract, ALU.mult).then_inc(n2_made, 1)
                    elif kind[:2] == "nX":
                        t = int(kind[2])
                        here = cur["par"] if t < 2 else prev
                        dve.wait_ge(rstd_made, TILES * (g if t < 2 else b) + 1 + t)
                        if t >= 2:
                            dve.wait_ge(unit_full, n_full(b, ("x", t - 2)))
                        nc.vector.tensor_scalar(nrm[:, t % 2, :], x2[here][:, t, :], nmv[:, t, 0:1], nrs[:, t:t + 1],
                                                ALU.subtract, ALU.mult).then_inc(xn_made, 1)
                    elif kind in ("out01", "out23"):
                        for t in (0, 1) if kind == "out01" else (2, 3):
                            evacuate(b - 1, t)
                    elif kind == "sq":
                        dve.wait_ge(relu_made, NFF * b + j + 1)
                        nc.vector.tensor_tensor(rbuf[:, j % 2, :], rbuf[:, j % 2, :], rbuf[:, j % 2, :], ALU.mult
                                                ).then_inc(square_made, 1)
                    elif kind == "lo":
                        dve.wait_ge(sqhi_made, NFF * b + j + 1)
                        nc.vector.tensor_tensor(qbuf[:, j % 2, LO, :], rbuf[:, j % 2, :], qbuf[:, j % 2, HI, :],
                                                ALU.subtract).then_inc(sqlo_made, 1)
                    elif kind == "scale":
                        dve.wait_ge(abs_done, 4 * j + 4)
                        if j < 4:
                            sc, n = scf[:, 4 * j:4 * j + 4], 4
                            link(nc.vector.tensor_scalar(sc, asum[:, j, :], 1.0 / D, EPS, ALU.mult, ALU.max))
                        else:
                            sc, n = spc[:, j - 4:j - 3], 1
                            link(nc.vector.tensor_reduce(psum4[:, j - 4:j - 3], asum[:, j, :], AX_X, ALU.add))
                            link(nc.vector.tensor_scalar(sc, psum4[:, j - 4:j - 3], 1.0 / HID, EPS, ALU.mult, ALU.max))
                        nc.vector.tensor_scalar(half[:, j % 2, 0:n], sc, 0.5, None, ALU.mult
                                                ).then_inc(scales_made, 1)
                        dve.wait_ge(scales_made, j + 1)
                    elif kind == "sides":
                        gr, i = j // 4, j % 4
                        bound = half[:, gr % 2, i if gr < 4 else 0:(i if gr < 4 else 0) + 1]
                        w = wring[:, gr % 2, i, :]
                        if j >= 2:
                            dve.wait_ge(tern_made, j - 1)
                        nc.vector.tensor_scalar(above[:, j % 2, :], w, bound, None, ALU.is_gt)
                        nc.vector.tensor_scalar(below[:, j % 2, :], w, -1.0, bound, ALU.mult, ALU.is_gt
                                                ).then_inc(sides_made, 1)
                    elif kind == "store" and j % 4 in DVE_STORES:
                        dve.wait_ge(tern_turned, j + 1)
                        nc.vector.tensor_copy(piece_place(j), piece_bank(j)).then_inc(dve_stored, 1)
                    elif kind == "uprep":
                        dve.wait_ge(lowrank_in, 16 * 7)
                        link(nc.vector.reciprocal(urs[:, :], scf[:, :]))
                        link(nc.vector.tensor_scalar(urs[:, :], urs[:, :], gatec[:, 0:1], None, ALU.mult))
                        link(nc.vector.tensor_tensor(u_s[:, :, :], u_s[:, :, :],
                                                     urs[:, :].unsqueeze(2).broadcast_to([P, NFF, RK]), ALU.mult))
                        link(nc.vector.tensor_copy(uhi[:, :, :], u_s[:, :, :]))
                        for i in range(4):
                            nc.vector.tensor_copy(unat[:, :, 2 * i, :], uhi[:, :, :])
                            last = nc.vector.tensor_tensor(unat[:, :, 2 * i + 1, :], u_s[:, :, :], uhi[:, :, :],
                                                           ALU.subtract)
                        last.then_inc(unat_made, 1)
                    elif kind == "diag":
                        dve.wait_ge(ident_made, 1)
                        for t in range(KD):
                            last = nc.vector.tensor_scalar(bvrep[:, t, :], ident[:, :], spc[:, t:t + 1], None, ALU.mult)
                        last.then_inc(diag_made, 1)
                    elif kind == "sprow_out":
                        dve.wait_ge(sprow_full, 1)
                        nc.vector.tensor_copy(sprow[:, :], banks["O0"][:, :]).then_inc(sprow_made, 1)
                        dve.wait_ge(sprow_made, 1)
                if not first and not (isinstance(b, int) and b == NG - 1):
                    assert chain["n"] == PER_BODY + (STATISTICS if isinstance(b, int) and b == 0 else 0)

            STATISTICS = 2 + 2
            PER_BODY = STATISTICS + 4 + 8 + 2
            run_bodies(dve, steps, "dve")
            for t in range(TILES):
                evacuate(NG - 1, t)
                if t % 2:
                    dve.wait_ge(y_made, 4 * (NG - 1) + t + 1)
                    nc.vector.tensor_tensor(x2[1][:, t, :], x2[1][:, t, :], ybuf[t], ALU.add
                                            ).then_inc(odd_y_added, 1)

        @block.tensor
        def _(pe):
            pe.wait_ge(ident_made, 1)

            def job(n):
                kind, c = JOBS[n]
                bank = banks[f"H{n % 2}"]
                if n >= 2:
                    job_read(pe, n - 2)
                if kind in ("wqT", "wkT", "wvT"):
                    if kind == "wqT":
                        pe.wait_ge(wq_in[c], 16)
                    elif kind == "wkT":
                        pe.wait_ge(gained, 1)
                    else:
                        pe.wait_ge(wv_in, 16)
                    w = {"wqT": Wq_s, "wkT": Wk_s, "wvT": Wv_s}[kind]
                    for k in range(KE):
                        mm = pe.transpose(bank[:, k * P:(k + 1) * P], w[:, c, k * P:(k + 1) * P], ident[:, :])
                elif kind == "bq":
                    pe.wait_ge(b1rep_made, 1)
                    for k in range(KD):
                        mm = pe.matmul(bank[:, :], bvrep[:, k, :], Wq_s[:, k, :], start=(k == 0), stop=(k == KD - 1))
                elif kind == "bv":
                    pe.wait_ge(vbias_in, 16 * 3)
                    for e in range(KE):
                        for k in range(KC):
                            mm = pe.matmul(bank[:, e:e + 1], Wv_s[:, k, e * P:(e + 1) * P], b2c[:, k:k + 1],
                                           start=(k == 0), stop=(k == KC - 1))
                elif kind == "M":
                    if c == 0:
                        for last in (KC - 2, KC - 1):
                            job_read(pe, JOBS.index(("wkT", last)))
                    for k in range(KE):
                        mm = pe.matmul(bank[:, 0:DC], WqT[:, k, c * P:(c + 1) * P], WkT[:, k, :],
                                       start=(k == 0), stop=(k == KE - 1))
                elif kind == "wvo":
                    if c == 0:
                        pe.wait_ge(wo_in, 16)
                        for last in (JOBS.index(("wvT", KC - 2)), JOBS.index(("wvT", KC - 1))):
                            job_read(pe, last)
                    for k in range(KE):
                        mm = pe.matmul(bank[:, :], WvT[:, k, c * P:(c + 1) * P], Wo_s[:, k, :],
                                       start=(k == 0), stop=(k == KE - 1))
                elif kind == "co":
                    job_read(pe, JOBS.index(("bv", 0)))
                    for k in range(KE):
                        mm = pe.matmul(bank[:, :], bvrep[:, k, :], Wo_s[:, k, :], start=(k == 0), stop=(k == KE - 1))
                elif kind == "fb":
                    pe.wait_ge(lowrank_in, 16 * 7)
                    for k in range(KD):
                        mm = pe.matmul(bank[:, k * 64:(k + 1) * 64], v_s[:, k * P:(k + 1) * P],
                                       fbT4[:, :, :].rearrange("s i r -> s (i r)"), start=True, stop=True)
                mm.then_inc(job_full, 1)

            def products(bank, pairs):
                for i, (w, m) in enumerate(pairs):
                    mm = pe.matmul(bank, w, m, start=(i == 0), stop=(i == len(pairs) - 1))
                return mm

            THREE = [(HI, HI), (HI, LO), (LO, HI)]

            def unit(b, un):
                kind, t = un
                name = bank_of(b, un)
                bank = banks[name]
                before = bank_before(b, un)
                cols = slice(t * P, (t + 1) * P)
                if isinstance(b, int) and b < 0 and name[0] == "H" and before is None:
                    job_read(pe, max(n for n in range(len(JOBS)) if f"H{n % 2}" == name))
                elif un in (("x", 2), ("x", 3)) and not (isinstance(b, int) and b == 0):
                    pe.wait_ge(relu_made, NFF * (b - 1) + NFF - 1 + (t == 3))
                elif before:
                    if before[1][0] == "s":
                        pe.wait_ge(unit_act, n_act(*before))
                    else:
                        pe.wait_ge(unit_dve, n_dve(*before))
                if kind in ("x", "n1T", "n2T"):
                    src, made = {"x": (nrm[:, t % 2, :], xn_made), "n1T": (nrm[:, t % 2, :], n1_made),
                                 "n2T": (ctxb[:, t, :], n2_made)}[kind]
                    pe.wait_ge(made, 4 * (b if kind == "x" else b + 1) + t + 1)
                    for k in range(KC if kind == "n2T" else KD):
                        mm = pe.transpose(bank[:, k * P:(k + 1) * P], src[:, k * P:(k + 1) * P], ident[:, :])
                elif kind == "L":
                    if isinstance(b, int) and b == 0:
                        job_read(pe, JOBS.index(("fb", 0)))
                    pe.wait_ge(unit_dve, n_dve(b, ("x", 3)))
                    mm = products(bank[:, :], [(FB[:, k, :], xnT[:, h, k, :]) for k in range(KD) for h in (HI, LO)])
                elif kind == "t":
                    if isinstance(b, int) and b < 0 and t == 0:
                        job_read(pe, JOBS.index(("M", KD - 1)))
                    pe.wait_ge(unit_dve, n_dve(b, ("n1T", 3)))
                    mm = products(bank[:, :], [(M[:, w, k, cols], n1T[:, m, k, :]) for k in range(KD) for w, m in THREE])
                elif kind == "s":
                    c = t // 2
                    if t == 0:
                        pe.wait_ge(unit_dve, n_dve(b, ("t", 2)))
                    mm = products(bank[:, 0:S], [(tT[:, w, k, cols], n2T[:, m, k, c * S:(c + 1) * S])
                                                 for k in range(KC) for w, m in THREE])
                elif kind == "w":
                    if t == 0:
                        pe.wait_ge(n2lo_made, 4 * (b + 2))
                        pe.wait_ge(unit_dve, n_dve(b, ("pT", 1)))
                    for c in range(2):
                        mm = products(bank[:, c * S:(c + 1) * S], [(n2rows[:, w, 2 * c + j, cols], pT[:, m, c, j, :])
                                                                   for j in range(2) for w, m in THREE])
                elif kind == "pT":
                    pe.wait_ge(unit_act, n_act(b, ("s", 2 * t + 1)))
                    for j in range(2):
                        for q in range(2):
                            mm = pe.transpose(bank[:, j * S + q * P:j * S + (q + 1) * P],
                                              pbuf[:, 2 * t + q, j * P:(j + 1) * P], ident[:, :])
                elif kind == "a":
                    if t == 0:
                        pe.wait_ge(unit_dve, n_dve(b, ("w", 2)))
                        if isinstance(b, int) and b < 0:
                            job_read(pe, JOBS.index(("wvo", KC - 1)))
                    mm = products(bank[:, :], [(tT[:, w, k, cols], Wvo[:, m, k, :]) for k in range(KC)
                                               for w, m in THREE])
                mm.then_inc(unit_full, 1)

            def turn_free(j):
                if j >= 4:
                    piece_stored(pe, j - 4)

            def down(b, j):
                pe.wait_ge(sqlo_made, NFF * b + j + 1)
                if j == 0:
                    if isinstance(b, int) and b == 0:
                        for k in range(4):
                            piece_stored(pe, PIECES - 4 + k)
                        pe.wait_ge(sprow_made, 1)
                    else:
                        pe.wait_ge(y_made, 4 * b)
                for t in range(TILES):
                    for h in (HI, LO):
                        mm = pe.matmul(banks[f"O{t}"][:, :], qbuf[:, j % 2, h, t * P:(t + 1) * P], projT[:, j, :],
                                       start=(j == 0 and h == HI), stop=(j == NFF - 1 and h == LO))
                mm.then_inc(down_full, 1)

            def steps(b, todo, odd=None):
                for st in todo:
                    kind, j = st if isinstance(st, tuple) else (st, None)
                    if kind in ("x", "L", "n1T", "n2T", "t", "s", "w", "pT", "a"):
                        unit(b, st)
                    elif kind == "job":
                        job(j)
                    elif kind == "up":
                        if j == 0:
                            pe.wait_ge(unit_dve, n_dve(b, ("x", 3)))
                        elif j >= 2:
                            pe.wait_ge(relu_made, NFF * b + j - 1)
                        for k in range(KD):
                            for h in (HI, LO):
                                pe.matmul(banks[f"H{j % 2}"][:, :], fcT[:, k, j * P:(j + 1) * P], xnT[:, h, k, :],
                                          start=(k == 0 and h == HI), stop=False)
                        if j == 0:
                            pe.wait_ge(unit_dve, n_dve(b, ("L", 0)))
                            if isinstance(b, int) and b == 0:
                                pe.wait_ge(ut_stored, 4)
                        pe.matmul(banks[f"H{j % 2}"][:, :], uT[:, j * P:(j + 1) * P], tstack[:, :],
                                  start=False, stop=True).then_inc(up_full, 1)
                    elif kind == "down":
                        down(b, j)
                    elif kind == "down-":
                        down(b - 1, j)
                    elif kind == "turn":
                        pe.wait_ge(tern_made, j + 1)
                        if j == 0:
                            pe.wait_ge(identb_made, 1)
                        turn_free(j)
                        if j >= 23:
                            pe.wait_ge(ut_stored, min(j - 22, 4))
                        ps = banks[f"O{j % 4}"][:, 0:256].bitcast(BF16)
                        for k in range(4):
                            mm = pe.transpose(ps[:, k * P:(k + 1) * P], tern[:, j % 4, k * P:(k + 1) * P], identb[:, :])
                        mm.then_inc(tern_turned, 1)
                    elif kind == "ut":
                        if j == 0:
                            pe.wait_ge(unat_made, 1)
                        turn_free(j + 23)
                        for i in range(4):
                            mm = pe.transpose(banks[f"O{(j + 23) % 4}"][:, i * P:(i + 1) * P],
                                              unat[:, 4 * j + i, :, :].rearrange("p i r -> p (i r)"), ident[:, :])
                        mm.then_inc(ut_full, 1)
                    elif kind == "sprow":
                        pe.wait_ge(diag_made, 1)
                        piece_stored(pe, PIECES - 4)
                        for t in range(KD):
                            mm = pe.matmul(banks["O0"][:, t * P:(t + 1) * P], ones[:, :], bvrep[:, t, :],
                                           start=True, stop=True)
                        mm.then_inc(sprow_full, 1)

            run_bodies(pe, steps, "pe")
            for t in range(TILES):
                for j in (NFF - 2, NFF - 1):
                    if t == 0:
                        pe.wait_ge(sqlo_made, NFF * (NG - 1) + j + 1)
                    for h in (HI, LO):
                        mm = pe.matmul(banks[f"O{t}"][:, :], qbuf[:, j % 2, h, t * P:(t + 1) * P], projT[:, j, :],
                                       start=False, stop=(j == NFF - 1 and h == LO))
                mm.then_inc(down_full, 1)


_INS = ['x', 'ctx_768', 'L0_xattn_ln1_g', 'L0_xattn_ln1_b', 'L0_xattn_ln2_g', 'L0_xattn_ln2_b', 'L0_xattn_Wq',
        'L0_xattn_bq', 'L0_xattn_Wk', 'L0_xattn_bk', 'L0_xattn_Wv', 'L0_xattn_bv', 'L0_xattn_Wo', 'L0_xattn_bo',
        'L0_ffn_fast_b', 'L0_ffn_w_fc', 'L0_ffn_w_proj', 'L0_ffn_u', 'L0_ffn_v', 'L0_ffn_gate']
_OUTS = [((16, 256, 512), 'float32')]


def kernel(**inputs):
    import numpy as _np
    import concourse.bacc as _bacc
    from concourse import mybir as _mybir
    from concourse.bass_utils import run_bass_kernel_spmd as _run

    nc = _bacc.Bacc("TRN2", target_bir_lowering=False, num_devices=1, dynamic_dma_scratch_size=1024)
    arrays, args = {}, []
    for name in _INS:
        a = _np.ascontiguousarray(inputs[name])
        arrays[f"in_{name}_dram"] = a
        args.append(nc.dram_tensor(f"in_{name}_dram", a.shape, _mybir.dt.from_np(a.dtype), kind="ExternalInput").ap())
    for i, (shape, dtype) in enumerate(_OUTS):
        dt = _mybir.dt.from_np(_np.dtype(dtype))
        args.append(nc.dram_tensor(f"out_{i}_dram", shape, dt, kind="ExternalOutput").ap())
    mk_xattn_ffn(nc, *args)
    r = _run(nc, [arrays], core_ids=[0])
    got = tuple(r.results[0][f"out_{i}_dram"] for i in range(len(_OUTS)))
    return got[0]
```
